# Optimizing a Trainium2 kernel written in Bass

```python
import numpy as np
import jax
import jax.numpy as jnp

def _softmax(x, axis=-1):
    return jax.nn.softmax(x, axis=axis)

def _gelu(x):
    return jax.nn.gelu(x, approximate=True)

def _silu(x):
    return jax.nn.silu(x)

def _sigmoid(x):
    return jax.nn.sigmoid(x)

def _layernorm(x, axis=-1, eps=1e-05):
    m = jnp.mean(x, axis=axis, keepdims=True)
    v = jnp.var(x, axis=axis, keepdims=True)
    return (x - m) / jnp.sqrt(v + eps)

def _scatter_add(tgt, idx, src, axis=0):
    return tgt.at[idx].add(src)

def _segment_sum(src, seg, n):
    return jax.ops.segment_sum(src, seg, n)
kernel_name = 'mk_gps_d1_gnn_r8_c353ad'

def setup_inputs(seed: int=0):
    np.random.seed(seed)
    _w = jnp.asarray

    def _rec_inputs():
        import jax
        import jax.numpy as jnp
        _gk = jax.random.key(seed)
        x = -0.0001126 + 1 * jax.random.normal(jax.random.fold_in(_gk, 1), (1250, 768), jnp.float32)
        _s = jax.random.randint(jax.random.fold_in(_gk, 2), (20000,), 0, 1250, jnp.int32)
        _d = jax.random.randint(jax.random.fold_in(_gk, 3), (20000,), 0, 1250, jnp.int32)
        _loop = jnp.arange(1250, dtype=jnp.int32)
        src = jnp.concatenate([_s, _d, _loop])
        dst = jnp.concatenate([_d, _s, _loop])
        _o = jnp.argsort(dst, stable=True)
        src = src[_o]
        dst = dst[_o]
        return (x, src, dst)
    x, src, dst = _rec_inputs()

    def _L0_gnn_setup():
        import jax, jax.numpy as jnp
        import numpy as np
        N, E, DM, H, L = (1250, 20000, 768, 8, 2)
        HD = DM // H
        LN_EPS = 1e-05
        SLOPE = 0.2

        def layer_norm(x, w, b):
            mu = jnp.mean(x, axis=-1, keepdims=True)
            var = jnp.mean(jnp.square(x - mu), axis=-1, keepdims=True)
            return (x - mu) * jax.lax.rsqrt(var + LN_EPS) * w + b

        def gatv2_layer(x, Ws, bs, Wd, bd, attn, src, dst):
            hs = (x @ Ws + bs).reshape(N, H, HD)
            hd = (x @ Wd + bd).reshape(N, H, HD)
            hs_e = hs[src]
            e = jax.nn.leaky_relu(hs_e + hd[dst], SLOPE)
            logits = jnp.einsum('ehd,hd->eh', e, attn)
            m = jax.ops.segment_max(logits, dst, num_segments=N)
            ex = jnp.exp(logits - m[dst])
            s = jax.ops.segment_sum(ex, dst, num_segments=N)
            alpha = ex / s[dst]
            out = jax.ops.segment_sum(alpha[..., None] * hs_e, dst, num_segments=N)
            return jax.nn.elu(out).reshape(N, DM)
        key = jax.random.key(seed)
        ks = jax.random.split(key, 12)
        xav = 1.0 / np.sqrt(DM)
        return {'x': jax.random.normal(ks[0], (N, DM), jnp.float32), 'Wsrc': jax.random.uniform(ks[1], (L, DM, DM), jnp.float32, -xav, xav), 'bsrc': jnp.zeros((L, DM), jnp.float32), 'Wdst': jax.random.uniform(ks[2], (L, DM, DM), jnp.float32, -xav, xav), 'bdst': jnp.zeros((L, DM), jnp.float32), 'attn': jax.random.normal(ks[3], (L, H, HD), jnp.float32) * (1.0 / np.sqrt(HD)), 'ln_w': jnp.ones((L, DM), jnp.float32), 'ln_b': jnp.zeros((L, DM), jnp.float32), 'on_w': jnp.ones((DM,), jnp.float32), 'on_b': jnp.zeros((DM,), jnp.float32), 'src': jax.random.randint(ks[4], (E,), 0, N, jnp.int32), 'dst': jax.random.randint(ks[5], (E,), 0, N, jnp.int32)}
    _L0_gnn_all = _L0_gnn_setup()
    _L0_gnn_in = {k: v for k, v in _L0_gnn_all.items() if k in ('Wsrc', 'bsrc', 'Wdst', 'bdst', 'attn', 'ln_w', 'ln_b', 'on_w', 'on_b')}
    del _L0_gnn_all

    def _L0_mix_setup():
        import jax, jax.numpy as jnp
        import numpy as np
        H = 12
        D = 64
        EPS = 1e-06

        def _phi(x):
            return jnp.where(x > 0, x + 1.0, jnp.exp(x))
        key = jax.random.key(seed)
        k1, k2, k3 = jax.random.split(key, 3)
        B, N, C = (4, 1024, 768)
        x = jax.random.normal(k1, (B, N, C), dtype=jnp.float32)
        W_qkv = jax.random.normal(k2, (C, 3 * C), dtype=jnp.float32) * C ** (-0.5)
        b_qkv = jnp.zeros((3 * C,), dtype=jnp.float32)
        W_out = jax.random.normal(k3, (C, C), dtype=jnp.float32) * C ** (-0.5)
        b_out = jnp.zeros((C,), dtype=jnp.float32)
        return {'x': x, 'W_qkv': W_qkv, 'b_qkv': b_qkv, 'W_out': W_out, 'b_out': b_out}
    _L0_mix_all = _L0_mix_setup()
    _L0_mix_in = {k: v for k, v in _L0_mix_all.items() if k in ('W_qkv', 'b_qkv', 'W_out', 'b_out')}
    del _L0_mix_all

    def _L0_ffn_setup():
        import jax, jax.numpy as jnp
        import numpy as np
        B, S, D_IN, D_HID, D_OUT = (32, 512, 768, 384, 768)
        key = jax.random.key(seed)
        k1, k2, k3, k4 = jax.random.split(key, 4)
        init_k = float(np.sqrt(1.0 / D_IN))
        init_k2 = float(np.sqrt(1.0 / D_HID))
        x = jax.random.normal(k1, (B, S, D_IN), dtype=jnp.float32)
        in_weight = jax.random.uniform(k2, (D_HID, D_IN), dtype=jnp.float32, minval=-init_k, maxval=init_k)
        in_bias = jax.random.uniform(k3, (D_HID,), dtype=jnp.float32, minval=-init_k, maxval=init_k)
        out_weight = jax.random.uniform(k4, (D_HID, D_OUT), dtype=jnp.float32, minval=-init_k2, maxval=init_k2)
        return {'x': x, 'in_weight': in_weight, 'in_bias': in_bias, 'out_weight': out_weight}
    _L0_ffn_all = _L0_ffn_setup()
    _L0_ffn_in = {k: v for k, v in _L0_ffn_all.items() if k in ('in_weight', 'in_bias', 'out_weight')}
    del _L0_ffn_all
    return {'x': x, 'src': src, 'dst': dst, 'L0_gnn_Wsrc': _L0_gnn_in['Wsrc'], 'L0_gnn_bsrc': _L0_gnn_in['bsrc'], 'L0_gnn_Wdst': _L0_gnn_in['Wdst'], 'L0_gnn_bdst': _L0_gnn_in['bdst'], 'L0_gnn_attn': _L0_gnn_in['attn'], 'L0_gnn_ln_w': _L0_gnn_in['ln_w'], 'L0_gnn_ln_b': _L0_gnn_in['ln_b'], 'L0_gnn_on_w': _L0_gnn_in['on_w'], 'L0_gnn_on_b': _L0_gnn_in['on_b'], 'L0_mix_W_qkv': _L0_mix_in['W_qkv'], 'L0_mix_b_qkv': _L0_mix_in['b_qkv'], 'L0_mix_W_out': _L0_mix_in['W_out'], 'L0_mix_b_out': _L0_mix_in['b_out'], 'L0_ffn_in_weight': _L0_ffn_in['in_weight'], 'L0_ffn_in_bias': _L0_ffn_in['in_bias'], 'L0_ffn_out_weight': _L0_ffn_in['out_weight']}

def reference(x, src, dst, L0_gnn_Wsrc, L0_gnn_bsrc, L0_gnn_Wdst, L0_gnn_bdst, L0_gnn_attn, L0_gnn_ln_w, L0_gnn_ln_b, L0_gnn_on_w, L0_gnn_on_b, L0_mix_W_qkv, L0_mix_b_qkv, L0_mix_W_out, L0_mix_b_out, L0_ffn_in_weight, L0_ffn_in_bias, L0_ffn_out_weight):
    import jax
    import jax.numpy as jnp

    def _L0_gnn_ref(x, Wsrc, bsrc, Wdst, bdst, attn, ln_w, ln_b, on_w, on_b, src, dst):
        import jax, jax.numpy as jnp
        import numpy as np
        N, E, DM, H, L = (1250, 20000, 768, 8, 2)
        HD = DM // H
        LN_EPS = 1e-05
        SLOPE = 0.2

        def layer_norm(x, w, b):
            mu = jnp.mean(x, axis=-1, keepdims=True)
            var = jnp.mean(jnp.square(x - mu), axis=-1, keepdims=True)
            return (x - mu) * jax.lax.rsqrt(var + LN_EPS) * w + b

        def gatv2_layer(x, Ws, bs, Wd, bd, attn, src, dst):
            hs = (x @ Ws + bs).reshape(N, H, HD)
            hd = (x @ Wd + bd).reshape(N, H, HD)
            hs_e = hs[src]
            e = jax.nn.leaky_relu(hs_e + hd[dst], SLOPE)
            logits = jnp.einsum('ehd,hd->eh', e, attn)
            m = jax.ops.segment_max(logits, dst, num_segments=N)
            ex = jnp.exp(logits - m[dst])
            s = jax.ops.segment_sum(ex, dst, num_segments=N)
            alpha = ex / s[dst]
            out = jax.ops.segment_sum(alpha[..., None] * hs_e, dst, num_segments=N)
            return jax.nn.elu(out).reshape(N, DM)
        h = x
        for l in range(L):
            h_new = gatv2_layer(h, Wsrc[l], bsrc[l], Wdst[l], bdst[l], attn[l], src, dst)
            h = layer_norm(h_new + h, ln_w[l], ln_b[l])
        return layer_norm(h, on_w, on_b)

    def _L0_mix_ref(x, W_qkv, b_qkv, W_out, b_out):
        import jax, jax.numpy as jnp
        import numpy as np
        H = 12
        D = 64
        EPS = 1e-06

        def _phi(x):
            return jnp.where(x > 0, x + 1.0, jnp.exp(x))
        B, N, C = x.shape
        qkv = x @ W_qkv + b_qkv
        qkv = qkv.reshape(B, N, 3, H, D).transpose(2, 0, 3, 1, 4)
        q, k, v = (qkv[0], qkv[1], qkv[2])
        qf = _phi(q)
        kf = _phi(k)
        kv = jnp.einsum('bhnd,bhne->bhde', kf.astype(jnp.float32), v.astype(jnp.float32)).astype(v.dtype)
        y_num = jnp.einsum('bhnd,bhde->bhne', qf, kv)
        z = kf.astype(jnp.float32).sum(axis=2)
        y_den = jnp.einsum('bhnd,bhd->bhn', qf, z.astype(qf.dtype))
        y_den = jnp.maximum(y_den[..., None], EPS)
        y = (y_num / y_den).transpose(0, 2, 1, 3).reshape(B, N, C)
        return y @ W_out + b_out

    def _L0_ffn_ref(x, in_weight, in_bias, out_weight):
        import jax, jax.numpy as jnp
        import numpy as np
        B, S, D_IN, D_HID, D_OUT = (32, 512, 768, 384, 768)
        lead = x.shape[:-1]
        xt = x.reshape(-1, in_weight.shape[1])
        h = jax.nn.gelu(jnp.einsum('td,hd->th', xt, in_weight) + in_bias, approximate=False)
        out = jnp.einsum('th,ho->to', h, out_weight)
        return out.reshape(*lead, out_weight.shape[1])
    xn = _layernorm(x, axis=-1)
    x = x + _L0_gnn_ref(xn, L0_gnn_Wsrc, L0_gnn_bsrc, L0_gnn_Wdst, L0_gnn_bdst, L0_gnn_attn, L0_gnn_ln_w, L0_gnn_ln_b, L0_gnn_on_w, L0_gnn_on_b, src, dst) + _L0_mix_ref(xn[None], L0_mix_W_qkv, L0_mix_b_qkv, L0_mix_W_out, L0_mix_b_out)[0]
    x = x + _L0_ffn_ref(_layernorm(x, axis=-1)[None], L0_ffn_in_weight, L0_ffn_in_bias, L0_ffn_out_weight)[0]
    return x

_drawn_inputs = setup_inputs


def setup_inputs(seed=0):
    import zlib

    import numpy as np

    out = dict(_drawn_inputs(seed))
    spreads = {'L0_gnn_bsrc': (0.0, 0.1),
     'L0_gnn_bdst': (0.0, 0.8),
     'L0_gnn_ln_w': (1.0, 0.2),
     'L0_gnn_ln_b': (0.0, 0.1),
     'L0_gnn_on_w': (1.0, 0.2),
     'L0_gnn_on_b': (0.0, 0.1),
     'L0_mix_b_qkv': (0.0, 0.1),
     'L0_mix_b_out': (0.0, 0.1)}
    factors = {'L0_gnn_Wdst': 4.868, 'L0_mix_W_qkv': 3.93, 'L0_ffn_in_bias': 8.0}
    for name, (base, spread) in spreads.items():
        noise = np.random.default_rng([zlib.crc32(name.encode()), seed]).standard_normal(out[name].shape)
        drawn = base * np.exp(spread * noise) if base else spread * noise
        out[name] = jnp.asarray(drawn.astype(out[name].dtype))
    for name, factor in factors.items():
        out[name] = (out[name] * factor).astype(out[name].dtype)
    return out
```

```python
from contextlib import ExitStack, contextmanager

import concourse.bass as bass
from concourse import mybir

F32, BF16, I32 = mybir.dt.float32, mybir.dt.bfloat16, mybir.dt.int32
ALU, ACT, AX = mybir.AluOpType, mybir.ActivationFunctionType, mybir.AxisListType

P = 128
N, D, E = 1250, 768, 41250
LAYERS, H = 2, 8
HD = D // H
NT = -(-N // P)
FULL = N // P
LAST = N - FULL * P
KC = D // P
HALF = D // 2
DX = D + H
HALFX = DX // 2
TC = KC // 2
TH = H // 2
G = 4
ME = G * P
ME_BITS = 9
UNROLL = 4
NG = -(-(E // ME + NT) // UNROLL)
NM = NG * UNROLL
NMX = NM + UNROLL
TG = UNROLL * G
T = NM * G
SPLIT = 3
BANK = 512
FAR = 1e30
TINY = 1e-30
SLOPE = 0.2
LN_EPS = 1e-5
MIX_EPS = 1e-6
MIX_D = 64
PAIRS = D // P
HID = 384
HC = HID // P
EP, ER = 125, E // 125
assert EP * ER == E and TC * P == TH * HD and TG * H == P and 2 * MIX_D == P and NMX <= P and 1 << ME_BITS == ME


class Link:

    def __init__(self, engine, sem, at=0):
        self.engine, self.sem, self.at = engine, sem, at

    def __call__(self, instruction):
        self.at = self.at + 1
        instruction.then_inc(self.sem, 1)
        self.engine.wait_ge(self.sem, self.at)


def allocator(nc, ctx):
    def sb(name, shape, dtype=F32):
        return ctx.enter_context(nc.sbuf_tensor(name, shape, dtype))

    return sb


@contextmanager
def signals(nc, names):
    with ExitStack() as ctx:
        sems = [ctx.enter_context(nc.semaphore(name)) for name in names]
        yield sems
        with nc.Block() as block:
            @block.sync
            def _(sp):
                for s in sems:
                    sp.sem_clear(s)


def rows_of(ap, t):
    return ap[:, bass.ds(t, 1), :].rearrange("p o d -> p (o d)")


def over(ap, n):
    return ap.unsqueeze(1).broadcast_to([ap.shape[0], n, ap.shape[1]])


class Norm:

    SIGNALS = ["stats_done", "var_ready", "root_ready", "order", "applied"]

    def __init__(self, sb, name, sems):
        self.stats = sb(name + "_stats", [P, 2 * NT, 6])
        self.mean = sb(name + "_mean", [P, NT])
        self.dev = sb(name + "_dev", [P, NT, 4])
        self.var = sb(name + "_var", [P, NT])
        self.rstd = sb(name + "_rstd", [P, NT])
        self.work = sb(name + "_work", [P, NT])
        self.stats_done, self.var_ready, self.root_ready, self.order, self.applied = sems

    @classmethod
    def names(cls, name):
        return [f"{name}_{s}" for s in cls.SIGNALS]

    def scalar(self, act):
        act.wait_ge(self.var_ready, 1)
        act.activation(self.rstd[:], self.var[:], ACT.Sqrt).then_inc(self.root_ready, 1)

    def vector(self, dve, data):
        step = Link(dve, self.order)
        with dve.Fori(0, NT) as t:
            for half in range(2):
                dve.bn_stats(rows_of(self.stats, t * 2 + half),
                             rows_of(data[:, :, half * HALF:(half + 1) * HALF], t)).then_inc(self.stats_done, 1)
        dve.wait_ge(self.stats_done, 2 * NT)
        groups = self.stats[:].rearrange("p (t h) (e k) -> p t (h e) k", h=2, k=3)
        means, spreads = groups[:, :, :, 1], groups[:, :, :, 2]
        step(dve.tensor_reduce(self.mean[:], means, AX.X, ALU.add))
        step(dve.tensor_scalar(self.mean[:], self.mean[:], 0.25, None, ALU.mult))
        step(dve.tensor_tensor(self.dev[:], means, self.mean[:].unsqueeze(2).broadcast_to([P, NT, 4]), ALU.subtract))
        step(dve.tensor_tensor(self.dev[:], self.dev[:], self.dev[:], ALU.mult))
        step(dve.tensor_reduce(self.var[:], self.dev[:], AX.X, ALU.add))
        step(dve.tensor_reduce(self.work[:], spreads, AX.X, ALU.add))
        step(dve.tensor_scalar(self.var[:], self.var[:], 0.25, LN_EPS, ALU.mult, ALU.add))
        step(dve.scalar_tensor_tensor(self.var[:], self.work[:], 1.0 / D, self.var[:], ALU.mult, ALU.add))
        dve.sem_inc(self.var_ready, 1)
        dve.wait_ge(self.root_ready, 1)
        step(dve.reciprocal(self.rstd[:], self.rstd[:]))
        step(dve.tensor_tensor(self.work[:], self.rstd[:], self.rstd[:], ALU.mult))
        step(dve.tensor_tensor(self.work[:], self.work[:], self.var[:], ALU.mult))
        step(dve.tensor_scalar(self.work[:], self.work[:], -0.5, 1.5, ALU.mult, ALU.add))
        step(dve.tensor_tensor(self.rstd[:], self.rstd[:], self.work[:], ALU.mult))
        with dve.Fori(0, NT) as t:
            dve.tensor_scalar(rows_of(data, t), rows_of(data, t), self.mean[:, bass.ds(t, 1)],
                              self.rstd[:, bass.ds(t, 1)], ALU.subtract, ALU.mult).then_inc(self.applied, 1)
        dve.wait_ge(self.applied, NT)


def load_and_norm(x, nc, nodes, ident, iota_p, iota_row, row_valid, head_mask, **_):
    with ExitStack() as ctx:
        x_loaded, pad_zero, made, *norm_sems = ctx.enter_context(signals(
            nc, ["x_loaded", "pad_zero", "const_made", *Norm.names("norm0")]))
        norm = Norm(allocator(nc, ctx), "norm0", norm_sems)
        with nc.Block() as block:
            @block.sync
            def _(sp):
                sp.dma_start(nodes[:, 0:FULL, :], x[0:FULL * P, :].rearrange("(t p) d -> p t d", p=P)).then_inc(x_loaded, 16)
                sp.wait_ge(pad_zero, 1)
                sp.dma_start(nodes[0:LAST, FULL, :], x[FULL * P:N, :]).then_inc(x_loaded, 16)

            @block.gpsimd
            def _(pool):
                pool.memset(ident[:], 0.0).then_inc(made, 1)
                pool.memset(row_valid[:], 1.0).then_inc(made, 1)
                pool.memset(head_mask[:], 1.0 - SLOPE).then_inc(made, 1)
                pool.wait_ge(made, 3)
                pool.affine_select(out=head_mask[:], in_=head_mask[:], compare_op=ALU.is_ge, fill=0.0, base=0,
                                   pattern=[[P, TC], [-HD, TH]], channel_multiplier=1).then_inc(made, 1)
                pool.wait_ge(made, 4)
                pool.affine_select(out=head_mask[:], in_=head_mask[:], compare_op=ALU.is_ge, fill=0.0, base=HD - 1,
                                   pattern=[[-P, TC], [HD, TH]], channel_multiplier=-1).then_inc(made, 1)
                pool.affine_select(out=ident[:], in_=ident[:], compare_op=ALU.not_equal, fill=1.0, base=0,
                                   pattern=[[-1, P]], channel_multiplier=1).then_inc(made, 1)
                pool.affine_select(out=row_valid[:], in_=row_valid[:], compare_op=ALU.is_ge, fill=0.0, base=N - 1,
                                   pattern=[[-P, NT]], channel_multiplier=-1).then_inc(made, 1)
                pool.iota(iota_p[:], [[0, 1]], base=0, channel_multiplier=1,
                          allow_small_or_imprecise_dtypes=True).then_inc(made, 1)
                pool.iota(iota_row[:], [[1, ME]], base=0, channel_multiplier=0,
                          allow_small_or_imprecise_dtypes=True).then_inc(made, 1)

            @block.scalar
            def _(act):
                norm.scalar(act)

            @block.vector
            def _(dve):
                dve.memset(nodes[:, FULL, :], 0.0).then_inc(pad_zero, 1)
                dve.wait_ge(x_loaded, 32)
                norm.vector(dve, nodes)


def index_edges(src, dst, nc, ident, iota_p, iota_row, src_index, dst_local, block_of, new_run, end_run,
                tile_flags, src_pad, dst_pad, local_rows, global_rows, block_list, **_):
    with ExitStack() as ctx:
        sb = allocator(nc, ctx)
        zeros = sb("ix_zeros", [1, ME], I32)
        before = sb("ix_before", [1, 1])
        dst_i, dst_f, junk = sb("ix_dst_i", [EP, ER], I32), sb("ix_dst_f", [EP, ER]), sb("ix_junk", [EP, ER])
        count, ones = sb("ix_count", [EP, NT]), sb("ix_ones", [EP, P])
        start = sb("ix_start", [P, NT + 1])
        first = sb("ix_first", [P, NT + 1])
        size, size_i, none = sb("ix_size", [P, NT]), sb("ix_size_i", [P, NT], I32), sb("ix_none", [P, NT])
        passed, step_to, part = sb("ix_passed", [P, NT - 1]), sb("ix_step", [P, NT - 1]), sb("ix_part", [P, NT - 1])
        blk, blk_i, shift = sb("ix_blk", [P, 1]), sb("ix_blk_i", [P, 1], I32), sb("ix_shift", [P, 1])
        base, base_i, valid, end = sb("ix_base", [P, 1]), sb("ix_base_i", [P, 1], I32), sb("ix_valid", [P, 1]), sb("ix_end", [P, 1])
        rows_i = sb("ix_rows_i", [NMX, 2, ME], I32)
        rows = sb("ix_rows", [NMX, 2, ME])
        mask, glob, local = sb("ix_mask", [NMX, ME]), sb("ix_glob", [NMX, ME]), sb("ix_local", [NMX, ME])
        local_b = sb("ix_local_b", [NMX, ME], BF16)
        around = sb("ix_around", [P, NG, P + 2])
        edge_of = sb("ix_edge_of", [H, 4, T])
        ps = ctx.enter_context(nc.psum_tensor("ix_ps", [P, 3, BANK], F32))
        (order, zero_made, padded, dst_loaded, counted, summed, base_made, lists_made, stored, listed,
         cols_ready, flags_loaded) = ctx.enter_context(signals(nc, ["ix_" + s for s in (
             "order", "zero_made", "padded", "dst_loaded", "counted", "summed", "base_made",
             "lists_made", "stored", "listed", "cols_ready", "flags_loaded")]))
        gathered = nc.alloc_semaphore("ix_gathered")
        with nc.Block() as block:
            @block.sync
            def _(sp):
                sp.dma_start(dst_i[:], dst.rearrange("(p e) -> p e", p=EP)).then_inc(dst_loaded, 16)
                for pad, edges in ((src_pad, src), (dst_pad, dst)):
                    sp.dma_start(pad[0:E].rearrange("(p e) -> p e", p=EP), edges.rearrange("(p e) -> p e", p=EP)).then_inc(padded, 16)
                sp.wait_ge(zero_made, 2)
                for pad in (src_pad, dst_pad):
                    sp.dma_start(pad[E:E + ME].rearrange("(o e) -> o e", o=1), zeros[:]).then_inc(padded, 16)
                sp.dma_start(global_rows[0:1].rearrange("(o e) -> o e", o=1), before[:]).then_inc(stored, 16)
                sp.wait_ge(lists_made, 3)
                sp.dma_start(global_rows[1:1 + NMX * ME].rearrange("(m e) -> m e", m=NMX), glob[:]).then_inc(stored, 16)
                sp.dma_start(local_rows, local_b[:]).then_inc(stored, 16)
                sp.dma_start(block_list.rearrange("(m o) -> m o", o=1), blk_i[0:NMX, :]).then_inc(stored, 16)
                sp.wait_ge(stored, 64)
                sp.dma_start(block_of[:], block_list.rearrange("(o m) -> o m", o=1)).then_inc(listed, 16)
                for h in range(H):
                    sp.dma_start(around[h * TG:(h + 1) * TG], bass.AP(
                        global_rows.tensor, 0, [[P, TG], [TG * P, NG], [1, P + 2]])).then_inc(flags_loaded, 16)
                for k, at in enumerate((0, 1, P, P + 1)):
                    sp.dma_start(edge_of[:, k, :], bass.AP(global_rows.tensor, at, [[0, H], [P, T]]), allow_slow_non_contiguous=True).then_inc(flags_loaded, 16)
                sp.wait_ge(listed, 16)

            @block.gpsimd
            def _(pool):
                pool.memset(zeros[:], 0).then_inc(zero_made, 1)
                pool.memset(before[:], -2.0).then_inc(zero_made, 1)
                pool.wait_ge(base_made, 1)
                pool.wait_ge(padded, 64)
                for k, pad in enumerate((src_pad, dst_pad)):
                    pool.indirect_dma_start(rows_i[:, k, :], None, pad.rearrange("(e o) -> e o", o=1),
                                            bass.IndirectOffsetOnAxis(base_i[0:NMX, 0:1], 0)).then_inc(gathered, 16)

            @block.tensor
            def _(pe):
                pe.wait_ge(counted, 1)
                pe.matmul(ps[:, 0, 0:NT], ones[:], count[:], start=True, stop=True).then_inc(summed, 1)
                pe.wait_ge(cols_ready, 2)
                for k, what in enumerate((rows[:, 0, :], local[:])):
                    for j in range(G):
                        pe.transpose(ps[:, 1 + k, j * P:j * P + NMX], what[:, j * P:(j + 1) * P],
                                     ident[0:NMX, 0:NMX]).then_inc(summed, 1)

            @block.vector
            def _(dve):
                step = Link(dve, order)
                dve.memset(ones[:], 1.0).then_inc(order, 1)
                dve.memset(none[:], 0.0).then_inc(order, 1)
                dve.memset(start[:, 0:1], 0.0).then_inc(order, 1)
                dve.memset(first[:, 0:1], 0.0).then_inc(order, 1)
                step.at = 4
                dve.wait_ge(dst_loaded, 16)
                step(dve.tensor_copy(dst_f[:], dst_i[:]))
                for b in range(NT):
                    step(dve.tensor_scalar(junk[:], dst_f[:], float((b + 1) * P), None, ALU.is_lt, ALU.add,
                                           accum_out=count[:, b:b + 1]))
                dve.sem_inc(counted, 1)
                dve.wait_ge(summed, 1)
                step(dve.tensor_copy(start[:, 1:], ps[:, 0, 0:NT]))
                step(dve.tensor_tensor(size[:], start[:, 1:], start[:, 0:NT], ALU.subtract))
                step(dve.tensor_scalar(size[:], size[:], float(ME - 1), None, ALU.add))
                step(dve.tensor_copy(size_i[:], size[:]))
                step(dve.tensor_scalar(size_i[:], size_i[:], ME_BITS, None, ALU.arith_shift_right))
                step(dve.tensor_copy(size[:], size_i[:]))
                step(dve.tensor_tensor_scan(first[:, 1:], none[:], size[:], 0.0, ALU.add, ALU.add))
                step(dve.tensor_scalar(passed[:], first[:, 1:NT], iota_p[:], None, ALU.is_le))
                step(dve.tensor_reduce(blk[:], passed[:], AX.X, ALU.add))
                step(dve.tensor_tensor(step_to[:], first[:, 1:NT], first[:, 0:NT - 1], ALU.subtract))
                step(dve.tensor_scalar(step_to[:], step_to[:], float(-ME), None, ALU.mult))
                step(dve.tensor_tensor(step_to[:], step_to[:], start[:, 1:NT], ALU.add))
                step(dve.tensor_tensor(step_to[:], step_to[:], start[:, 0:NT - 1], ALU.subtract))
                step(dve.tensor_tensor(part[:], passed[:], step_to[:], ALU.mult))
                step(dve.tensor_reduce(base[:], part[:], AX.X, ALU.add))
                step(dve.tensor_scalar(shift[:], iota_p[:], float(ME), None, ALU.mult))
                step(dve.tensor_tensor(base[:], base[:], shift[:], ALU.add))
                step(dve.tensor_scalar(base[:], base[:], float(E), None, ALU.min))
                step(dve.tensor_copy(base_i[:], base[:]))
                dve.sem_inc(base_made, 1)
                step(dve.tensor_tensor(step_to[:], start[:, 2:], start[:, 1:NT], ALU.subtract))
                step(dve.tensor_tensor(part[:], passed[:], step_to[:], ALU.mult))
                step(dve.tensor_reduce(end[:], part[:], AX.X, ALU.add))
                step(dve.tensor_tensor(end[:], end[:], start[:, 1:2], ALU.add))
                step(dve.tensor_tensor(valid[:], end[:], base[:], ALU.subtract))
                step(dve.tensor_copy(blk_i[:], blk[:]))
                dve.sem_inc(lists_made, 1)
                step(dve.tensor_scalar(shift[:], blk[:], float(-P), 1.0, ALU.mult, ALU.add))
                step(dve.tensor_scalar(mask[:], iota_row[0:NMX], valid[0:NMX], None, ALU.is_lt))
                dve.wait_ge(gathered, 32)
                step(dve.tensor_copy(rows[:], rows_i[:]))
                step(dve.tensor_tensor(rows[:, 0, :], rows[:, 0, :], mask[:], ALU.mult))
                step(dve.scalar_tensor_tensor(glob[:], rows[:, 1, :], 1.0, mask[:], ALU.add, ALU.mult))
                step(dve.tensor_scalar(glob[:], glob[:], -1.0, None, ALU.add))
                dve.sem_inc(lists_made, 1)
                step(dve.scalar_tensor_tensor(local[:], rows[:, 1, :], shift[0:NMX], mask[:], ALU.add, ALU.mult))
                step(dve.tensor_scalar(local[:], local[:], -1.0, None, ALU.add))
                dve.sem_inc(cols_ready, 2)
                step(dve.tensor_copy(local_b[:], local[:]))
                dve.sem_inc(lists_made, 1)
                dve.wait_ge(summed, 1 + 2 * G)
                for k, columns in enumerate((src_index, dst_local)):
                    step(dve.tensor_copy(columns[:].rearrange("p m j -> p j m"),
                                         ps[:, 1 + k, :].rearrange("p (j m) -> p j m", j=G)[:, :, 0:NMX]))
                dve.wait_ge(flags_loaded, 16 * (H + 4))
                for flags, beside, alone in ((new_run, 0, 0), (end_run, 2, P - 1)):
                    step(dve.tensor_tensor(flags[:], around[:, :, 1:P + 1], around[:, :, beside:P + beside], ALU.not_equal))
                    step(dve.tensor_scalar(flags[:], flags[:], -FAR, None, ALU.mult))
                    step(dve.memset(flags[:, :, alone:alone + 1], -FAR))
                for k, (a, b) in enumerate(((0, 2), (0, 1), (1, 3), (2, 3))):
                    step(dve.tensor_tensor(tile_flags[:, k, :], edge_of[:, a, :], edge_of[:, b, :], ALU.not_equal))
                step(dve.tensor_scalar(tile_flags[:], tile_flags[:], -FAR, None, ALU.mult))


def persistent(nc, sb):
    def dram(name, shape, dtype=F32):
        return nc.dram_tensor(name, shape, dtype).ap()

    return dict(
        nc=nc,
        ident=sb("ident", [P, P]),
        iota_p=sb("iota_p", [P, 1]),
        iota_row=sb("iota_row", [P, ME]),
        nodes=sb("nodes", [P, NT, D]),
        head_mask=sb("head_mask", [P, TC, TH]),
        row_valid=sb("row_valid", [P, NT]),
        src_index=sb("src_index", [P, NMX, G], I32),
        dst_local=sb("dst_local", [P, NMX, G]),
        block_of=sb("block_of", [1, NMX], I32),
        new_run=sb("new_run", [P, NG, P]),
        end_run=sb("end_run", [P, NG, P]),
        tile_flags=sb("tile_flags", [H, 4, T]),
        src_pad=dram("src_pad", [E + ME], I32),
        dst_pad=dram("dst_pad", [E + ME], I32),
        local_rows=dram("local_rows", [NMX, ME], BF16),
        global_rows=dram("global_rows", [1 + NMX * ME]),
        block_list=dram("block_list", [NMX], I32),
        table=dram("table", [NT * P, DX]),
        x_mix=dram("x_mix", [P, NT * D]),
        tails=dram("tails", [2, NG, H, TG]),
        carries=dram("carries", [2, NG, H, TG]),
    )


def project(layer, Wsrc, bsrc, Wdst, bdst, attn, attn_relu, dst_rows, sems, nc, ident, nodes, table, **_):
    with ExitStack() as ctx:
        sb = allocator(nc, ctx)
        weights = [sb(f"pr_w{s}", [P, KC, D]) for s in range(2)]
        bias = [sb(f"pr_b{s}", [P, D]) for s in range(2)]
        attn_lin = sb("pr_attn_lin", [P, D])
        node = [sb(f"pr_node{b}", [P, D]) for b in range(2)]
        node_t = [sb(f"pr_node_t{b}", [P, KC, P]) for b in range(2)]
        src_row = [sb(f"pr_src_row{b}", [P, DX]) for b in range(2)]
        dst_row = sb("pr_dst_row", [P, DX])
        rest = sb("pr_rest", [P, DX])
        prod = sb("pr_prod", [P, D])
        turned = ctx.enter_context(nc.psum_tensor("pr_turned", [P, 2 * BANK], F32))
        src_ps = ctx.enter_context(nc.psum_tensor("pr_src_ps", [P, 2, BANK], F32))
        dst_ps = ctx.enter_context(nc.psum_tensor("pr_dst_ps", [P, 2, BANK], F32))
        (w_loaded, attn_loaded, attn_ready, node_ready, turned_done, node_t_ready, src_done, dst_done, src_taken,
         dst_taken, row_ready, row_stored, row_free, order, split_ready, split_done) = names = [nc.alloc_semaphore("pr_" + s) for s in (
             "w_loaded", "attn_loaded", "attn_ready", "node_ready", "turned_done", "node_t_ready", "src_done", "dst_done",
             "src_taken", "dst_taken", "row_ready", "row_stored", "row_free", "order", "split_ready", "split_done")]
        sems += names
        STEPS = 8
        with nc.Block() as block:
            @block.sync
            def _(sp):
                sp.dma_start(attn_lin[:], attn.rearrange("l h d -> l (h d)")[bass.ds(layer, 1), :].broadcast_to([P, D])).then_inc(attn_loaded, 16)
                for s, (w, b) in enumerate(((Wsrc, bsrc), (Wdst, bdst))):
                    sp.dma_start(weights[s][:], w.rearrange("l k n -> (l k) n")[bass.ds(layer * D, D), :]
                                 .rearrange("(c p) n -> p c n", p=P)).then_inc(w_loaded, 16)
                    sp.dma_start(bias[s][:], b[bass.ds(layer, 1), :].broadcast_to([P, D])).then_inc(w_loaded, 16)
                with sp.Fori(0, NT // 2) as i:
                    for b in range(2):
                        t = i * 2 + b
                        sp.wait_ge(row_ready, t + 1)
                        sp.dma_start(table[bass.ds(t * P, P), :], src_row[b][:]).then_inc(row_stored, 16)
                        sp.wait_ge(row_stored, 16 * t + 16)
                        sp.sem_inc(row_free, 1)

            @block.scalar
            def _(act):
                act.wait_ge(attn_loaded, 16)
                act.activation(attn_relu[:], attn_lin[:], ACT.Copy, scale=1.0 - SLOPE).then_inc(attn_ready, 1)
                act.wait_ge(attn_ready, 1)
                act.activation(attn_lin[:], attn_lin[:], ACT.Copy, scale=SLOPE).then_inc(attn_ready, 1)
                with act.Fori(0, NT // 2) as i:
                    for b in range(2):
                        t = i * 2 + b
                        act.activation(node[b][:], rows_of(nodes, t), ACT.Copy).then_inc(node_ready, 1)
                        act.wait_ge(turned_done, t + 1)
                        act.activation(node_t[b][:], turned[:, 0:D].rearrange("p (c n) -> p c n", c=KC), ACT.Copy).then_inc(node_t_ready, 1)
                        act.wait_ge(split_ready, 3 * t + 1)
                        act.activation(dst_rows[:, bass.ds(t, 1), 0, :].rearrange("p o d -> p (o d)"), dst_row[:], ACT.Copy).then_inc(split_done, 1)
                        act.wait_ge(split_ready, 3 * t + 2)
                        act.activation(dst_rows[:, bass.ds(t, 1), 1, :].rearrange("p o d -> p (o d)"), rest[:], ACT.Copy).then_inc(split_done, 1)
                        act.wait_ge(split_ready, 3 * t + 3)
                        act.activation(dst_rows[:, bass.ds(t, 1), 2, :].rearrange("p o d -> p (o d)"), rest[:], ACT.Copy).then_inc(split_done, 1)

            @block.tensor
            def _(pe):
                pe.wait_ge(w_loaded, 64)
                with pe.Fori(0, NT // 2) as i:
                    for b in range(2):
                        t = i * 2 + b
                        pe.wait_ge(node_ready, t + 1)
                        for c in range(KC):
                            last = pe.transpose(turned[:, c * P:(c + 1) * P], node[b][:, c * P:(c + 1) * P], ident[:])
                        last.then_inc(turned_done, 1)
                        pe.wait_ge(node_t_ready, t + 1)
                        for w, ps, taken, done in ((weights[0], src_ps, src_taken, src_done), (weights[1], dst_ps, dst_taken, dst_done)):
                            pe.wait_ge(taken, t + 1)
                            for half in range(2):
                                for c in range(KC):
                                    last = pe.matmul(ps[:, half, 0:HALF], node_t[b][:, c, :],
                                                     w[:, c, half * HALF:(half + 1) * HALF], start=c == 0, stop=c == KC - 1)
                            last.then_inc(done, 1)

            @block.vector
            def _(dve):
                dve.sem_inc(src_taken, 1)
                dve.sem_inc(dst_taken, 1)
                dve.sem_inc(row_free, 2)
                dve.wait_ge(w_loaded, 64)
                dve.wait_ge(attn_ready, 2)
                with dve.Fori(0, NT // 2) as i:
                    for b in range(2):
                        t = i * 2 + b
                        step = Link(dve, order, t * STEPS)
                        dve.wait_ge(row_free, t + 1)
                        for row, ps, offset, taken, done in ((src_row[b], src_ps, bias[0], src_taken, src_done),
                                                             (dst_row, dst_ps, bias[1], dst_taken, dst_done)):
                            dve.wait_ge(done, t + 1)
                            step(dve.tensor_tensor(row[:, 0:D].rearrange("p (s d) -> p s d", s=2), ps[:, :, 0:HALF],
                                                   offset[:].rearrange("p (s d) -> p s d", s=2), ALU.add))
                            dve.sem_inc(taken, 1)
                            step(dve.tensor_tensor(prod[:], row[:, 0:D], attn_lin[:], ALU.mult))
                            step(dve.tensor_reduce(row[:, D:DX], prod[:].rearrange("p (h d) -> p h d", h=H), AX.X, ALU.add))
                            if row is dst_row:
                                dve.sem_inc(split_ready, 1)
                            else:
                                dve.sem_inc(row_ready, 1)
                        whole = dst_row
                        for s in range(SPLIT - 1):
                            dve.wait_ge(split_done, 3 * t + s + 1)
                            step(dve.tensor_tensor(rest[:], whole[:], dst_rows[:, bass.ds(t, 1), s, :].rearrange("p o d -> p (o d)"), ALU.subtract))
                            dve.sem_inc(split_ready, 1)
                            whole = rest
                        dve.wait_ge(split_done, 3 * t + 3)


AHEAD = 2


def landed(layer, b, rounds):
    return 16 * G * (layer * (NG + (b < AHEAD)) + rounds)


def logits_of_edges(layer, table, attn, local_rows, src_index, block_of, iota_p, ident, head_mask, attn_relu, dst_rows, logits,
                    sems, nc, **_):
    with ExitStack() as ctx:
        sb = allocator(nc, ctx)
        rows = [sb(f"lg_rows{b}", [P, G, DX]) for b in range(UNROLL)]
        index = [sb(f"lg_index{b}", [P, G], I32) for b in range(UNROLL)]
        local = [sb(f"lg_local{b}", [P, ME], BF16) for b in range(UNROLL)]
        place = [sb(f"lg_place{b}", [P, ME], BF16) for b in range(UNROLL)]
        relu = [sb(f"lg_relu{b}", [P, TC, ME]) for b in range(2)]
        attn_col = sb("lg_attn_col", [P, TC])
        attn_diag = sb("lg_attn_diag", [P, TC, TH])
        turned = [ctx.enter_context(nc.psum_tensor(f"lg_turned{c}", [P, BANK], F32)) for c in range(TC)]
        ends = [ctx.enter_context(nc.psum_tensor(f"lg_ends{j}", [P, BANK], F32)) for j in range(G)]
        products = ctx.enter_context(nc.psum_tensor("lg_products", [P, G, TH], F32))
        (index_ready, index_seen, local_free, place_ready, turned_done, turned_relu, products_done, products_taken, ends_done, ends_free,
         added, rows_free, relu_done, pool_done, dve_done, reduced, attn_loaded, attn_ready) = names = [nc.alloc_semaphore("lg_" + s) for s in (
             "index_ready", "index_seen", "local_free", "place_ready", "turned_done", "turned_relu", "products_done", "products_taken",
             "ends_done", "ends_free", "added", "rows_free", "relu_done", "pool_done", "dve_done", "reduced", "attn_loaded", "attn_ready")]
        gathered = [nc.alloc_semaphore(f"lg_gathered{b}") for b in range(UNROLL)]
        local_loaded = [nc.alloc_semaphore(f"lg_local_loaded{b}") for b in range(UNROLL)]
        sems += [*names, *local_loaded]
        POOL = 2
        with nc.Block() as block:
            @block.sync
            def _(sp):
                sp.dma_start(attn_col[:], attn.rearrange("l h d -> (l h d)")[bass.ds(layer * D, HALF)].rearrange("(c p) -> p c", p=P),
                             allow_slow_non_contiguous=True).then_inc(attn_loaded, 16)

                def load_local(m, b):
                    sp.wait_ge(local_free, m + 1)
                    sp.dma_start(local[b][:], local_rows[bass.ds(m, 1), :].broadcast_to([P, ME])).then_inc(local_loaded[b], 16)

                with sp.Fori(0, NG) as i:
                    for b in range(UNROLL):
                        load_local(i * UNROLL + b, b)
                for b in range(AHEAD):
                    load_local(NM + b, b)
                for b in range(UNROLL):
                    sp.wait_ge(local_loaded[b], 16 * (NG + (b < AHEAD)))

            @block.gpsimd
            def _(pool):
                def gather(m, b):
                    pool.wait_ge(rows_free, m + 1)
                    pool.tensor_copy(index[b][:], rows_of(src_index, m)).then_inc(index_ready, 1)
                    pool.wait_ge(index_ready, m + 1)
                    pool.sem_inc(index_seen, 1)
                    for j in range(G):
                        pool.indirect_dma_start(rows[b][:, j, :], None, table,
                                                bass.IndirectOffsetOnAxis(index[b][:, j:j + 1], 0)).then_inc(gathered[b], 16)

                for m in range(AHEAD):
                    gather(m, m)
                with pool.Fori(0, NG) as i:
                    for b in range(UNROLL):
                        m = i * UNROLL + b
                        gather(m + AHEAD, (b + AHEAD) % UNROLL)
                        pool.wait_ge(relu_done, m + 1)
                        pool.tensor_tensor(rows[b][:, 0:POOL, HALF:D], rows[b][:, 0:POOL, HALF:D], over(attn_relu[:, HALF:], POOL),
                                           ALU.mult).then_inc(pool_done, 1)
                for b in range(UNROLL):
                    pool.wait_ge(gathered[b], landed(layer, b, NG + (b < AHEAD)))

            @block.scalar
            def _(act):
                act.sem_inc(turned_relu, TC)
                with act.Fori(0, NG) as i:
                    for b in range(UNROLL):
                        m = i * UNROLL + b
                        act.wait_ge(products_done, m + 1)
                        for c in range(TC):
                            act.wait_ge(turned_done, m * TC + c + 1)
                            act.activation(relu[b % 2][:, c, :], turned[c][:], ACT.Relu).then_inc(turned_relu, 1)
                        act.wait_ge(added, G * m + POOL)
                        act.activation(rows[b][:, 0:POOL, HALF:D], rows[b][:, 0:POOL, HALF:D], ACT.Relu).then_inc(relu_done, 1)

            @block.tensor
            def _(pe):
                def part(block_at, s, at, n):
                    return dst_rows[:, bass.ds(block_at, 1), s, at:at + n].rearrange("p o d -> p (o d)")

                def turn(m, b, round, block_at):
                    pe.wait_ge(gathered[b], landed(layer, b, round + 1))
                    pe.wait_ge(place_ready, m + 1)
                    for c in range(TC):
                        pe.wait_ge(turned_relu, m * TC + c + 1)
                        for s in range(SPLIT):
                            pe.matmul(turned[c][:], part(block_at, s, c * P, P), place[b][:], start=s == 0, stop=False)
                        for j in range(G):
                            last = pe.matmul(turned[c][:, j * P:(j + 1) * P], rows[b][:, j, c * P:(c + 1) * P], ident[:],
                                             is_transpose=True, start=False, stop=j == G - 1)
                        last.then_inc(turned_done, 1)

                def sum_with_attn(m, b):
                    pe.wait_ge(turned_relu, (m + 2) * TC)
                    pe.wait_ge(products_taken, m + 1)
                    for j in range(G):
                        for c in range(TC):
                            last = pe.matmul(products[:, j, :], relu[b % 2][:, c, j * P:(j + 1) * P], attn_diag[:, c, :],
                                             start=c == 0, stop=c == TC - 1)
                    last.then_inc(products_done, 1)

                def ends_of(m, b, block_at):
                    for j in range(G):
                        pe.wait_ge(ends_free, m * G + j + 1)
                        for s in range(SPLIT):
                            last = pe.matmul(ends[j][:, 0:DX - HALF], place[b][:, j * P:(j + 1) * P], part(block_at, s, HALF, DX - HALF),
                                             start=s == 0, stop=s == SPLIT - 1)
                        last.then_inc(ends_done, 1)

                def block_at(m):
                    return pe.value_load(block_of[0:1, bass.ds(m, 1)], min_val=0, max_val=NT - 1)

                pe.sem_inc(products_done, 2)
                pe.wait_ge(attn_ready, 1)
                first = block_at(0)
                turn(0, 0, 0, first)
                ends_of(0, 0, first)
                with pe.Fori(0, NG) as i:
                    for b in range(UNROLL):
                        m = i * UNROLL + b
                        n = (b + 1) % UNROLL
                        at = block_at(m + 1)
                        turn(m + 1, n, i + (b + 1) // UNROLL, at)
                        sum_with_attn(m, b)
                        ends_of(m + 1, n, at)

            @block.vector
            def _(dve):
                def build_place(m, b, round):
                    dve.wait_ge(local_loaded[b], 16 * (round + 1))
                    dve.tensor_scalar(place[b][:], local[b][:], iota_p[:], None, ALU.is_equal).then_inc(place_ready, 1)
                    dve.wait_ge(place_ready, m + 1)
                    dve.sem_inc(local_free, 1)

                def add_ends(m, b, round):
                    dve.wait_ge(gathered[b], landed(layer, b, round + 1))
                    for j in range(G):
                        dve.wait_ge(ends_done, m * G + j + 1)
                        row = rows[b][:, j, HALF:DX]
                        dve.tensor_tensor(row, ends[j][:, 0:DX - HALF], row, ALU.add).then_inc(added, 1)
                    dve.wait_ge(added, m * G + G)
                    dve.sem_inc(ends_free, G)
                    dve.scalar_tensor_tensor(rows[b][:, POOL:, HALF:D], rows[b][:, POOL:, HALF:D], 0.0, over(attn_relu[:, HALF:], G - POOL),
                                             ALU.max, ALU.mult).then_inc(dve_done, 1)

                def reduce(m, i, b):
                    out = logits[:, bass.ds(i, 1), :, b * G:(b + 1) * G].rearrange("p o h j -> p j (o h)")
                    dve.wait_ge(products_done, m + 3)
                    dve.tensor_tensor(out[:, :, 0:TH], products[:], rows[b][:, :, D:D + TH], ALU.add).then_inc(products_taken, 1)
                    dve.wait_ge(dve_done, m + 1)
                    dve.wait_ge(pool_done, m + 1)
                    dve.tensor_reduce(out[:, :, TH:], rows[b][:, :, HALF:D].rearrange("p j (h d) -> p j h d", d=HD), AX.X, ALU.add).then_inc(reduced, 1)
                    dve.wait_ge(reduced, 2 * m + 1)
                    dve.tensor_tensor(out[:, :, TH:], out[:, :, TH:], rows[b][:, :, D + TH:DX], ALU.add).then_inc(reduced, 1)
                    dve.wait_ge(products_taken, m + 2)
                    dve.wait_ge(reduced, 2 * m + 2)
                    dve.sem_inc(rows_free, 1)

                dve.wait_ge(attn_loaded, 16)
                dve.tensor_tensor(attn_diag[:], head_mask[:], attn_col[:].unsqueeze(2).broadcast_to([P, TC, TH]), ALU.mult).then_inc(attn_ready, 1)
                dve.sem_inc(local_free, UNROLL)
                dve.sem_inc(rows_free, UNROLL)
                dve.sem_inc(ends_free, G)
                dve.sem_inc(products_taken, 1)
                build_place(0, 0, 0)
                build_place(1, 1, 0)
                add_ends(0, 0, 0)
                with dve.Fori(0, NG) as i:
                    for b in range(UNROLL):
                        m = i * UNROLL + b
                        build_place(m + 2, (b + 2) % UNROLL, i + (b + 2) // UNROLL)
                        add_ends(m + 1, (b + 1) % UNROLL, i + (b + 1) // UNROLL)
                        reduce(m, i, b)
                dve.wait_ge(dve_done, NM + 1)


def softmax_weights(logits, ident, new_run, end_run, tile_flags, tails, carries, sems, nc, **_):
    with ExitStack() as ctx:
        sb = allocator(nc, ctx)
        turned, left, right = sb("sm_turned", [P, NG, P]), sb("sm_left", [P, NG, P]), sb("sm_right", [P, NG, P])
        tail, kept = sb("sm_tail", [P, 2, NG]), sb("sm_kept", [P, 2, NG])
        tail_t, carry_t = sb("sm_tail_t", [2 * NG, P]), sb("sm_carry_t", [2 * NG, P])
        runs = sb("sm_runs", [H, 2, T])
        through = sb("sm_through", [H, 2, T])
        carry = sb("sm_carry", [H, 2, T])
        QUADS = -(-NG // 4)
        ps = ctx.enter_context(nc.psum_tensor("sm_ps", [P, QUADS, BANK], F32))
        ps_tail = ctx.enter_context(nc.psum_tensor("sm_ps_tail", [P, BANK], F32))
        ps_carry = ctx.enter_context(nc.psum_tensor("sm_ps_carry", [P, BANK], F32))
        (filled, taken, tails_ready, tail_done, tail_ready, tails_moved, runs_ready, carry_ready, carry_stored, carries_moved,
         carry_done, shifted, exps, back, order, written) = names = [nc.alloc_semaphore("sm_" + s) for s in (
             "filled", "taken", "tails_ready", "tail_done", "tail_ready", "tails_moved", "runs_ready", "carry_ready", "carry_stored",
             "carries_moved", "carry_done", "shifted", "exps", "back", "order", "written")]
        sems += names

        def flat(ap):
            return ap.rearrange("p g e -> p (g e)")

        def quad(ap, q):
            n = min(4, NG - 4 * q)
            return ap[:, 4 * q:4 * q + n], n * P

        with nc.Block() as block:
            @block.tensor
            def _(pe):
                for g in range(NG):
                    last = pe.transpose(ps[:, g // 4, g % 4 * P:(g % 4 + 1) * P], logits[:, g].rearrange("p h t -> p (h t)"), ident[:])
                    if g % 4 == 3 or g == NG - 1:
                        last.then_inc(filled, 1)
                pe.wait_ge(tails_ready, 1)
                pe.transpose(ps_tail[0:2 * NG, 0:P], tail[:].rearrange("p k g -> p (k g)"), ident[:]).then_inc(tail_done, 1)
                pe.wait_ge(carries_moved, 16)
                pe.transpose(ps_carry[:, 0:2 * NG], carry_t[:], ident[0:2 * NG, 0:2 * NG]).then_inc(carry_done, 1)
                for g in range(NG):
                    if g % 4 == 0:
                        pe.wait_ge(exps, g // 4 + 1)
                    last = pe.transpose(ps[:, g // 4, g % 4 * P:(g % 4 + 1) * P], turned[:, g, :], ident[:])
                    if g % 4 == 3 or g == NG - 1:
                        last.then_inc(back, 1)

            @block.scalar
            def _(act):
                for q in range(QUADS):
                    act.wait_ge(filled, q + 1)
                    to, n = quad(turned, q)
                    act.activation(flat(to), ps[:, q, 0:n], ACT.Copy).then_inc(taken, 1)
                act.wait_ge(tail_done, 1)
                act.activation(tail_t[:], ps_tail[0:2 * NG, 0:P], ACT.Copy).then_inc(tail_ready, 1)
                for q in range(QUADS):
                    if q == 0:
                        act.wait_ge(shifted, 1)
                    to, n = quad(turned, q)
                    act.activation(flat(to), flat(to), ACT.Exp).then_inc(exps, 1)
                for q in range(QUADS):
                    act.wait_ge(back, q + 1)
                    to, n = quad(logits, q)
                    act.activation(to.rearrange("p g h t -> p (g h t)"), ps[:, q, 0:n], ACT.Copy).then_inc(written, 1)

            @block.sync
            def _(sp):
                sp.wait_ge(tail_ready, 1)
                sp.dma_start(tails.rearrange("k g h t -> (k g) (h t)"), tail_t[:]).then_inc(tails_moved, 16)
                sp.wait_ge(tails_moved, 16)
                for k in range(2):
                    sp.dma_start(runs[:, k, :].rearrange("h (g t) -> h g t", t=TG), tails[k].rearrange("g h t -> h g t")).then_inc(runs_ready, 16)
                sp.wait_ge(carry_ready, 1)
                for k in range(2):
                    sp.dma_start(carries[k].rearrange("g h t -> h g t"), carry[:, k, :].rearrange("h (g t) -> h g t", t=TG)).then_inc(carry_stored, 16)
                sp.wait_ge(carry_stored, 32)
                sp.dma_start(carry_t[:], carries.rearrange("k g h t -> (k g) (h t)")).then_inc(carries_moved, 16)
                sp.wait_ge(carries_moved, 16)

            @block.vector
            def _(dve):
                step = Link(dve, order)

                def running():
                    step(dve.tensor_tensor_scan(flat(left[:]), flat(new_run[:]), flat(turned[:]), -FAR, ALU.add, ALU.max))
                    step(dve.tensor_tensor_scan(flat(right[:])[:, ::-1], flat(end_run[:])[:, ::-1], flat(turned[:])[:, ::-1],
                                                -FAR, ALU.add, ALU.max))

                dve.wait_ge(taken, QUADS)
                running()
                step(dve.tensor_copy(tail[:, 0, :], left[:, :, P - 1]))
                step(dve.tensor_copy(tail[:, 1, :], right[:, :, 0]))
                dve.sem_inc(tails_ready, 1)
                step(dve.tensor_copy(kept[:, 0, :], turned[:, :, 0]))
                step(dve.tensor_copy(kept[:, 1, :], turned[:, :, P - 1]))
                dve.wait_ge(runs_ready, 32)
                step(dve.tensor_tensor_scan(through[:, 0, :], tile_flags[:, 0, :], runs[:, 0, :], -FAR, ALU.add, ALU.max))
                step(dve.tensor_tensor_scan(through[:, 1, ::-1], tile_flags[:, 2, ::-1], runs[:, 1, ::-1], -FAR, ALU.add, ALU.max))
                step(dve.memset(carry[:, 0, 0:1], -FAR))
                step(dve.memset(carry[:, 1, T - 1:T], -FAR))
                step(dve.tensor_tensor(carry[:, 0, 1:], through[:, 0, 0:T - 1], tile_flags[:, 1, 1:], ALU.add))
                step(dve.tensor_tensor(carry[:, 1, 0:T - 1], through[:, 1, 1:], tile_flags[:, 3, 0:T - 1], ALU.add))
                dve.sem_inc(carry_ready, 1)
                dve.wait_ge(carry_done, 1)
                for k, at in enumerate((0, P - 1)):
                    step(dve.tensor_tensor(turned[:, :, at], ps_carry[:, k * NG:(k + 1) * NG], turned[:, :, at], ALU.max))
                running()
                step(dve.tensor_tensor(left[:], left[:], right[:], ALU.max))
                step(dve.tensor_copy(turned[:, :, 0], kept[:, 0, :]))
                step(dve.tensor_copy(turned[:, :, P - 1], kept[:, 1, :]))
                step(dve.tensor_tensor(turned[:], turned[:], left[:], ALU.subtract))
                dve.sem_inc(shifted, 1)
                dve.wait_ge(written, QUADS)


def sum_messages(layer, weights, sums, table, src_index, dst_local, block_of, iota_row, sems, nc, **_):
    with ExitStack() as ctx:
        sb = allocator(nc, ctx)
        rows = [sb(f"ms_rows{b}", [P, G, DX]) for b in range(UNROLL)]
        index = [sb(f"ms_index{b}", [P, G], I32) for b in range(UNROLL)]
        place = [sb(f"ms_place{b}", [P, G, P]) for b in range(UNROLL)]
        total = [ctx.enter_context(nc.psum_tensor(f"ms_total{b}", [P, 2, BANK], F32)) for b in range(2)]
        (index_ready, index_seen, rows_free, place_ready, weighted, behind, totalled, cleared, added) = names = [nc.alloc_semaphore("ms_" + s) for s in (
            "index_ready", "index_seen", "rows_free", "place_ready", "weighted", "behind", "totalled", "cleared", "added")]
        gathered = [nc.alloc_semaphore(f"ms_gathered{b}") for b in range(UNROLL)]
        sems += names
        with nc.Block() as block:
            @block.gpsimd
            def _(pool):
                pool.memset(sums[:], 0.0).then_inc(cleared, 1)

                def gather(m, b):
                    pool.wait_ge(rows_free, m + 1)
                    pool.tensor_copy(index[b][:], rows_of(src_index, m)).then_inc(index_ready, 1)
                    pool.wait_ge(index_ready, m + 1)
                    pool.sem_inc(index_seen, 1)
                    for j in range(G):
                        pool.indirect_dma_start(rows[b][:, j, :], None, table,
                                                bass.IndirectOffsetOnAxis(index[b][:, j:j + 1], 0)).then_inc(gathered[b], 16)

                for m in range(AHEAD):
                    gather(m, m)
                with pool.Fori(0, NG) as i:
                    for b in range(UNROLL):
                        gather(i * UNROLL + b + AHEAD, (b + AHEAD) % UNROLL)
                for b in range(UNROLL):
                    pool.wait_ge(gathered[b], landed(layer, b, NG + (b < AHEAD)))

            def weights_of(i, b):
                return weights[:, bass.ds(i, 1), :, b * G:(b + 1) * G].rearrange("p o h j -> p j (o h)")

            @block.scalar
            def _(act):
                with act.Fori(0, NG) as i:
                    for b in range(UNROLL):
                        act.wait_ge(gathered[b], landed(layer, b, i + 1))
                        act.activation(rows[b][:, :, D:DX], weights_of(i, b), ACT.Copy).then_inc(behind, 1)

            @block.tensor
            def _(pe):
                pe.sem_inc(rows_free, UNROLL)
                with pe.Fori(0, NG) as i:
                    for b in range(UNROLL):
                        m = i * UNROLL + b
                        pe.wait_ge(place_ready, m + 1)
                        pe.wait_ge(weighted, m + 1)
                        pe.wait_ge(behind, m + 1)
                        pe.wait_ge(added, m + 1)
                        for j in range(G):
                            for half in range(2):
                                last = pe.matmul(total[b % 2][:, half, 0:HALFX], place[b][:, j, :],
                                                 rows[b][:, j, half * HALFX:(half + 1) * HALFX], start=j == 0, stop=j == G - 1)
                        last.then_inc(totalled, 1)
                        pe.wait_ge(totalled, m + 1)
                        pe.sem_inc(rows_free, 1)

            @block.vector
            def _(dve):
                def prepare(m, i, b, round):
                    dve.tensor_tensor(place[b][:], over(iota_row[:, 0:P], G),
                                      rows_of(dst_local, m).unsqueeze(2).broadcast_to([P, G, P]), ALU.is_equal).then_inc(place_ready, 1)
                    dve.wait_ge(gathered[b], landed(layer, b, round + 1))
                    features = rows[b][:, :, 0:D].rearrange("p j (h d) -> p j h d", h=H)
                    dve.tensor_tensor(features, features, weights_of(i, b).unsqueeze(3).broadcast_to([P, G, H, HD]), ALU.mult).then_inc(weighted, 1)

                def add_total(m, b):
                    block_at = dve.value_load(block_of[0:1, bass.ds(m, 1)], min_val=0, max_val=NT - 1)
                    into = sums[:, bass.ds(block_at, 1), :].rearrange("p o (s d) -> p (o s) d", s=2)
                    dve.wait_ge(totalled, m + 1)
                    dve.wait_ge(added, m + 2)
                    dve.tensor_tensor(into, total[b % 2][:, :, 0:HALFX], into, ALU.add).then_inc(added, 1)

                dve.wait_ge(cleared, 1)
                dve.sem_inc(added, 2)
                prepare(0, 0, 0, 0)
                with dve.Fori(0, NG) as i:
                    for b in range(UNROLL):
                        m = i * UNROLL + b
                        n = (b + 1) // UNROLL
                        prepare(m + 1, i + n, (b + 1) % UNROLL, i + n)
                        add_total(m, b)
                dve.wait_ge(added, NM + 2)
                dve.wait_ge(weighted, NM + 1)
                dve.wait_ge(place_ready, NM + 1)


def end_layer(layer, sums, ln_w, ln_b, sems, nc, nodes, **_):
    with ExitStack() as ctx:
        sb = allocator(nc, ctx)
        norm = Norm(sb, "norm1", [nc.alloc_semaphore(s) for s in Norm.names("norm1")])
        gain, offset = sb("el_gain", [P, D]), sb("el_offset", [P, D])
        mean, bend = sb("el_mean", [P, NT, D]), sb("el_bend", [P, NT, D])
        inverse = sb("el_inverse", [P, NT, H])
        loaded, order, below, exp_done = names = [nc.alloc_semaphore("el_" + s) for s in ("loaded", "order", "below", "exp_done")]
        sems += [*names, norm.stats_done, norm.var_ready, norm.root_ready, norm.order, norm.applied]
        with nc.Block() as block:
            @block.sync
            def _(sp):
                sp.dma_start(gain[:], ln_w[bass.ds(layer, 1), :].broadcast_to([P, D])).then_inc(loaded, 16)
                sp.dma_start(offset[:], ln_b[bass.ds(layer, 1), :].broadcast_to([P, D])).then_inc(loaded, 16)

            @block.scalar
            def _(act):
                act.wait_ge(below, 1)
                act.activation(bend[:], bend[:], ACT.Exp).then_inc(exp_done, 1)
                norm.scalar(act)

            @block.vector
            def _(dve):
                step = Link(dve, order)
                step(dve.tensor_scalar(inverse[:], sums[:, :, D:DX], TINY, None, ALU.max))
                step(dve.reciprocal(inverse[:], inverse[:]))
                step(dve.tensor_tensor(mean[:].rearrange("p t (h d) -> p t h d", h=H),
                                       sums[:, :, 0:D].rearrange("p t (h d) -> p t h d", h=H),
                                       inverse[:].unsqueeze(3).broadcast_to([P, NT, H, HD]), ALU.mult))
                step(dve.tensor_scalar(bend[:], mean[:], 0.0, None, ALU.min))
                dve.sem_inc(below, 1)
                dve.wait_ge(exp_done, 1)
                step(dve.scalar_tensor_tensor(mean[:], mean[:], 0.0, bend[:], ALU.max, ALU.add))
                step(dve.scalar_tensor_tensor(nodes[:], mean[:], -1.0, nodes[:], ALU.add, ALU.add))
                norm.vector(dve, nodes)
                dve.wait_ge(loaded, 32)
                step(dve.tensor_tensor(nodes[:], nodes[:], over(gain[:], NT), ALU.mult))
                step(dve.tensor_tensor(nodes[:], nodes[:], over(offset[:], NT), ALU.add))


def attention_layers(Wsrc, bsrc, Wdst, bdst, attn, ln_w, ln_b, k):
    nc, sems = k["nc"], []
    with nc.Fori(0, LAYERS) as layer:
        with ExitStack() as ctx:
            sb = allocator(nc, ctx)
            logits = sb("logits", [P, NG + 1, H, TG])
            spare = nc.alloc_semaphore("spare_cleared")
            sems.append(spare)
            with nc.Block() as block:
                @block.vector
                def _(dve):
                    dve.memset(logits[:, NG], 0.0).then_inc(spare, 1)
                    dve.wait_ge(spare, 1)
            with ExitStack() as inner:
                sb = allocator(nc, inner)
                attn_relu = sb("attn_relu", [P, D])
                dst_rows = sb("dst_rows", [P, NT, SPLIT, DX], BF16)
                project(layer, Wsrc, bsrc, Wdst, bdst, attn, attn_relu, dst_rows, sems, **k)
                logits_of_edges(layer, attn=attn, attn_relu=attn_relu, dst_rows=dst_rows, logits=logits, sems=sems, **k)
            softmax_weights(logits=logits, sems=sems, **k)
            sums = allocator(nc, ctx)("sums", [P, NT, DX])
            sum_messages(layer, weights=logits, sums=sums, sems=sems, **k)
            end_layer(layer, sums, ln_w, ln_b, sems, **k)
        with nc.Block() as block:
            @block.sync
            def _(sp):
                for s in sems:
                    sp.sem_clear(s)


def mix(x, W_qkv, b_qkv, W_out, b_out, nc, ident, nodes, row_valid, x_mix, **_):
    W_KV = 2 * D
    with ExitStack() as ctx:
        sb = allocator(nc, ctx)
        nodes_t = sb("mx_nodes_t", [P, KC, NT * P])
        kv_bias = sb("mx_kv_bias", [P, W_KV])
        kv = sb("mx_kv", [P, PAIRS, P + 1])
        with ExitStack() as inner:
            sb = allocator(nc, inner)
            w = sb("mx_w", [P, KC, W_KV])
            node = [sb(f"mx_node{b}", [P, D]) for b in range(2)]
            node_t = [sb(f"mx_node_t{b}", [P, KC, P]) for b in range(2)]
            key, key_low, key_phi = sb("mx_key", [P, D]), sb("mx_key_low", [P, D]), [sb(f"mx_key_phi{b}", [P, D]) for b in range(2)]
            value = [sb(f"mx_value{b}", [P, PAIRS, P + 1]) for b in range(2)]
            turned = inner.enter_context(nc.psum_tensor("mx_turned", [P, 2 * BANK], F32))
            key_ps = inner.enter_context(nc.psum_tensor("mx_key_ps", [P, 2, BANK], F32))
            value_ps = inner.enter_context(nc.psum_tensor("mx_value_ps", [P, 2, BANK], F32))
            kv_ps = inner.enter_context(nc.psum_tensor("mx_kv_ps", [P, 2, BANK], F32))
            (w_loaded, node_ready, turned_done, turned_free, node_t_ready, key_done, key_taken, low_ready, exp_done, value_done,
             value_taken, kv_in, kv_done, kv_taken, order, cleared) = inner.enter_context(signals(nc, ["mx_" + s for s in (
                 "w_loaded", "node_ready", "turned_done", "turned_free", "node_t_ready", "key_done", "key_taken", "low_ready",
                 "exp_done", "value_done", "value_taken", "kv_in", "kv_done", "kv_taken", "order", "cleared")]))
            STEPS = 7
            with nc.Block() as block:
                @block.sync
                def _(sp):
                    sp.dma_start(w[:], W_qkv[:, D:].rearrange("(c p) n -> p c n", p=P)).then_inc(w_loaded, 16)
                    sp.dma_start(kv_bias[:], b_qkv[D:].rearrange("(o n) -> o n", o=1).broadcast_to([P, W_KV])).then_inc(w_loaded, 16)
                    sp.wait_ge(w_loaded, 32)

                @block.scalar
                def _(act):
                    act.sem_inc(turned_free, 1)
                    with act.Fori(0, NT // 2) as i:
                        for b in range(2):
                            t = i * 2 + b
                            act.activation(node[b][:], rows_of(nodes, t), ACT.Copy).then_inc(node_ready, 1)
                            act.wait_ge(turned_done, t + 1)
                            from_ps = turned[:, 0:D].rearrange("p (c n) -> p c n", c=KC)
                            act.activation(node_t[b][:], from_ps, ACT.Copy).then_inc(node_t_ready, 1)
                            act.activation(nodes_t[:, :, bass.ds(t * P, P)], from_ps, ACT.Copy).then_inc(turned_free, 1)
                            act.wait_ge(low_ready, t + 1)
                            act.activation(key_low[:], key_low[:], ACT.Exp).then_inc(exp_done, 1)

                @block.tensor
                def _(pe):
                    pe.wait_ge(w_loaded, 32)
                    with pe.Fori(0, NT // 2) as i:
                        for b in range(2):
                            t = i * 2 + b
                            pe.wait_ge(node_ready, t + 1)
                            pe.wait_ge(turned_free, t + 1)
                            for c in range(KC):
                                last = pe.transpose(turned[:, c * P:(c + 1) * P], node[b][:, c * P:(c + 1) * P], ident[:])
                            last.then_inc(turned_done, 1)
                            pe.wait_ge(node_t_ready, t + 1)
                            for s, (ps, taken, done) in enumerate(((key_ps, key_taken, key_done), (value_ps, value_taken, value_done))):
                                pe.wait_ge(taken, t + 1)
                                for half in range(2):
                                    at = s * D + half * HALF
                                    for c in range(KC):
                                        last = pe.matmul(ps[:, half, 0:HALF], node_t[b][:, c, :], w[:, c, at:at + HALF],
                                                         start=c == 0, stop=c == KC - 1)
                                last.then_inc(done, 1)
                            pe.wait_ge(kv_in, t + 1)
                            pe.wait_ge(kv_taken, t + 1)
                            for pair in range(PAIRS):
                                at = pair % 3 * (P + 1)
                                last = pe.matmul(kv_ps[:, pair // 3, at:at + P + 1], key_phi[b][:, pair * P:(pair + 1) * P],
                                                 value[b][:, pair, :], start=True, stop=True)
                            last.then_inc(kv_done, 1)

                @block.vector
                def _(dve):
                    for b in range(2):
                        dve.memset(value[b][:, :, P:], 1.0).then_inc(cleared, 1)
                    dve.memset(kv[:], 0.0).then_inc(cleared, 1)
                    for free in (key_taken, value_taken, kv_taken):
                        dve.sem_inc(free, 1)
                    dve.wait_ge(cleared, 3)
                    dve.wait_ge(w_loaded, 32)
                    with dve.Fori(0, NT // 2) as i:
                        for b in range(2):
                            t = i * 2 + b
                            step = Link(dve, order, t * STEPS)
                            dve.wait_ge(key_done, t + 1)
                            step(dve.tensor_tensor(key[:].rearrange("p (s d) -> p s d", s=2), key_ps[:, :, 0:HALF],
                                                   kv_bias[:, 0:D].rearrange("p (s d) -> p s d", s=2), ALU.add))
                            dve.sem_inc(key_taken, 1)
                            step(dve.tensor_scalar(key_low[:], key[:], 0.0, None, ALU.min))
                            dve.sem_inc(low_ready, 1)
                            dve.wait_ge(value_done, t + 1)
                            for half in range(2):
                                at = D + half * HALF
                                step(dve.tensor_tensor(value[b][:, half * 3:half * 3 + 3, 0:P],
                                                       value_ps[:, half, 0:HALF].rearrange("p (a d) -> p a d", a=3),
                                                       kv_bias[:, at:at + HALF].rearrange("p (a d) -> p a d", a=3), ALU.add))
                            dve.sem_inc(value_taken, 1)
                            dve.wait_ge(exp_done, t + 1)
                            step(dve.scalar_tensor_tensor(key_phi[b][:], key[:], 0.0, key_low[:], ALU.max, ALU.add))
                            step(dve.tensor_scalar(key_phi[b][:], key_phi[b][:], row_valid[:, bass.ds(t, 1)], None, ALU.mult))
                            dve.sem_inc(kv_in, 1)
                            dve.wait_ge(kv_done, t + 1)
                            into = kv[:].rearrange("p (s a) d -> p s (a d)", s=2)
                            step(dve.tensor_tensor(into, kv_ps[:, :, 0:3 * (P + 1)], into, ALU.add))
                            dve.sem_inc(kv_taken, 1)
        mixed_t = allocator(nc, ctx)("mx_mixed_t", [P, PAIRS, NT * P])
        with ExitStack() as inner:
            sb = allocator(nc, inner)
            bias = sb("mx_q_bias", [P, PAIRS])
            wq = [sb(f"mx_wq{b}", [P, KC, P]) for b in range(2)]
            pair_kv = [sb(f"mx_pair_kv{b}", [P, P]) for b in range(2)]
            pair_sum = [sb(f"mx_pair_sum{b}", [P, P]) for b in range(2)]
            low, high, query = ([sb(f"mx_{s}{b}", [P, BANK]) for b in range(2)] for s in ("low", "high", "query"))
            den = [sb(f"mx_den{b}", [P, BANK]) for b in range(2)]
            q_ps, num_ps, den_ps = ([inner.enter_context(nc.psum_tensor(f"mx_{s}_ps{b}", [P, BANK], F32)) for b in range(2)]
                                    for s in ("q", "num", "den"))
            (bias_loaded, q_done, q_low, q_exp, q_ready, weighed, out_ready, pair_ready, q_taken, out_taken, order2, wq_free, zeroed) = inner.enter_context(signals(nc, ["mx2_" + s for s in (
                    "bias_loaded", "q_done", "q_low", "q_exp", "q_ready", "weighed", "out_ready", "pair_ready", "q_taken", "out_taken",
                    "order", "wq_free", "zeroed")]))
            wq_loaded = inner.enter_context(signals(nc, [f"mx2_wq_loaded{b}" for b in range(2)]))
            CUTS = [(at, min(BANK, NT * P - at)) for at in range(0, NT * P, BANK)]
            CH = len(CUTS)
            STEPS = 4 + 6 * CH
            with nc.Block() as block:
                @block.sync
                def _(sp):
                    sp.dma_start(bias[:], b_qkv[0:D].rearrange("(f p) -> p f", p=P), allow_slow_non_contiguous=True).then_inc(bias_loaded, 16)
                    with sp.Fori(0, PAIRS // 2) as i:
                        for b in range(2):
                            f = i * 2 + b
                            sp.wait_ge(wq_free, f + 1)
                            sp.dma_start(wq[b][:], W_qkv[:, bass.ds(f * P, P)].rearrange("(c p) n -> p c n", p=P)).then_inc(wq_loaded[b], 16)
                    for b in range(2):
                        sp.wait_ge(wq_loaded[b], 16 * (PAIRS // 2))

                @block.tensor
                def _(pe):
                    pe.sem_inc(wq_free, 2)
                    with pe.Fori(0, PAIRS // 2) as i:
                        for b in range(2):
                            f = i * 2 + b
                            pe.wait_ge(wq_loaded[b], 16 * (i + 1))
                            pe.wait_ge(pair_ready, f + 1)
                            for n, (at, size) in enumerate(CUTS):
                                r = (b * CH + n) % 2
                                pe.wait_ge(q_taken, f * CH + n + 1)
                                for c in range(KC):
                                    last = pe.matmul(q_ps[r][:, 0:size], wq[b][:, c, :], nodes_t[:, c, at:at + size], start=c == 0, stop=c == KC - 1)
                                last.then_inc(q_done, 1)
                                pe.wait_ge(q_ready, f * CH + n + 1)
                                pe.wait_ge(out_taken, f * CH + n + 1)
                                pe.matmul(num_ps[r][:, 0:size], pair_kv[b][:], query[r][:, 0:size], start=True, stop=True)
                                pe.matmul(den_ps[r][:, 0:size], pair_sum[b][:], query[r][:, 0:size], start=True, stop=True).then_inc(weighed, 1)
                            pe.wait_ge(weighed, f * CH + CH)
                            pe.sem_inc(wq_free, 1)

                @block.scalar
                def _(act):
                    with act.Fori(0, PAIRS // 2) as i:
                        for b in range(2):
                            f = i * 2 + b
                            for n, (at, size) in enumerate(CUTS):
                                r = (b * CH + n) % 2
                                act.wait_ge(q_low, f * CH + n + 1)
                                act.activation(low[r][:, 0:size], low[r][:, 0:size], ACT.Exp).then_inc(q_exp, 1)

                @block.vector
                def _(dve):
                    dve.sem_inc(q_taken, 2)
                    dve.sem_inc(out_taken, 2)
                    for b in range(2):
                        dve.memset(pair_kv[b][:], 0.0).then_inc(zeroed, 1)
                        dve.memset(pair_sum[b][:], 0.0).then_inc(zeroed, 1)
                    dve.wait_ge(zeroed, 4)
                    dve.wait_ge(bias_loaded, 16)
                    with dve.Fori(0, PAIRS // 2) as i:
                        for b in range(2):
                            f = i * 2 + b
                            step = Link(dve, order2, f * STEPS)
                            for a in range(0, P, MIX_D):
                                head = kv[a:a + MIX_D, bass.ds(f, 1), :].rearrange("p o d -> p (o d)")
                                step(dve.tensor_copy(pair_kv[b][a:a + MIX_D, a:a + MIX_D], head[:, a:a + MIX_D]))
                                step(dve.tensor_copy(pair_sum[b][a:a + MIX_D, a:a + MIX_D], head[:, P:P + 1].broadcast_to([MIX_D, MIX_D])))
                            dve.sem_inc(pair_ready, 1)
                            for n, (at, size) in enumerate(CUTS):
                                r = (b * CH + n) % 2
                                dve.wait_ge(q_done, f * CH + n + 1)
                                step(dve.tensor_scalar(low[r][:, 0:size], q_ps[r][:, 0:size], bias[:, bass.ds(f, 1)], 0.0, ALU.add, ALU.min))
                                dve.sem_inc(q_low, 1)
                                step(dve.tensor_scalar(high[r][:, 0:size], q_ps[r][:, 0:size], bias[:, bass.ds(f, 1)], 0.0, ALU.add, ALU.max))
                                dve.sem_inc(q_taken, 1)
                                dve.wait_ge(q_exp, f * CH + n + 1)
                                step(dve.tensor_tensor(query[r][:, 0:size], high[r][:, 0:size], low[r][:, 0:size], ALU.add))
                                dve.sem_inc(q_ready, 1)
                                dve.wait_ge(weighed, f * CH + n + 1)
                                step(dve.tensor_scalar(den[r][:, 0:size], den_ps[r][:, 0:size], MIX_EPS, None, ALU.max))
                                step(dve.reciprocal(den[r][:, 0:size], den[r][:, 0:size]))
                                step(dve.tensor_tensor(mixed_t[:, bass.ds(f, 1), at:at + size].rearrange("p o n -> p (o n)"),
                                                       num_ps[r][:, 0:size], den[r][:, 0:size], ALU.mult))
                                dve.sem_inc(out_taken, 1)
        total = nodes_t[:].rearrange("p c n -> p (c n)").rearrange("p (t d) -> p t d", t=NT)
        with ExitStack() as inner:
            sb = allocator(nc, inner)
            w = sb("mx_wo", [P, KC, D])
            bias = sb("mx_bo", [P, D])
            part = [sb(f"mx_part{b}", [P, KC, P]) for b in range(2)]
            ps = [inner.enter_context(nc.psum_tensor(f"mx_out_ps{b}", [P, 2, BANK], F32)) for b in range(2)]
            w_loaded, x_loaded, part_ready, done, taken, order3, zeroed3, stored = inner.enter_context(signals(nc, ["mx3_" + s for s in (
                "w_loaded", "x_loaded", "part_ready", "done", "taken", "order", "zeroed", "stored")]))
            with nc.Block() as block:
                @block.sync
                def _(sp):
                    sp.dma_start(w[:], W_out.rearrange("(c p) n -> p c n", p=P)).then_inc(w_loaded, 16)
                    sp.dma_start(bias[:], b_out.rearrange("(o n) -> o n", o=1).broadcast_to([P, D])).then_inc(w_loaded, 16)
                    sp.dma_start(total[:, 0:FULL, :], x[0:FULL * P, :].rearrange("(t p) d -> p t d", p=P)).then_inc(x_loaded, 16)
                    sp.wait_ge(zeroed3, 1)
                    sp.dma_start(total[0:LAST, FULL, :], x[FULL * P:N, :]).then_inc(x_loaded, 16)
                    sp.wait_ge(order3, 2 * NT)
                    sp.dma_start(x_mix, total.rearrange("p t d -> p (t d)")).then_inc(stored, 16)
                    sp.wait_ge(stored, 16)

                @block.scalar
                def _(act):
                    with act.Fori(0, NT // 2) as i:
                        for b in range(2):
                            t = i * 2 + b
                            act.wait_ge(taken, t + 1)
                            act.activation(part[b][:], mixed_t[:, :, bass.ds(t * P, P)], ACT.Copy).then_inc(part_ready, 1)

                @block.tensor
                def _(pe):
                    pe.wait_ge(w_loaded, 32)
                    with pe.Fori(0, NT // 2) as i:
                        for b in range(2):
                            t = i * 2 + b
                            pe.wait_ge(part_ready, t + 1)
                            for half in range(2):
                                for c in range(KC):
                                    last = pe.matmul(ps[b][:, half, 0:HALF], part[b][:, c, :], w[:, c, half * HALF:(half + 1) * HALF],
                                                     start=c == 0, stop=c == KC - 1)
                            last.then_inc(done, 1)

                @block.vector
                def _(dve):
                    dve.memset(total[:, FULL, :], 0.0).then_inc(zeroed3, 1)
                    dve.sem_inc(taken, 2)
                    dve.wait_ge(x_loaded, 32)
                    dve.wait_ge(w_loaded, 32)
                    with dve.Fori(0, NT // 2) as i:
                        for b in range(2):
                            t = i * 2 + b
                            step = Link(dve, order3, t * 2)
                            row = rows_of(total, t)
                            step(dve.tensor_tensor(row, row, bias[:], ALU.add))
                            dve.wait_ge(done, t + 1)
                            halves = row.rearrange("p (s d) -> p s d", s=2)
                            step(dve.tensor_tensor(halves, ps[b][:, :, 0:HALF], halves, ALU.add))
                            dve.sem_inc(taken, 1)


def finish(on_w, on_b, in_weight, in_bias, out_weight, out, nc, ident, nodes, x_mix, **_):
    with ExitStack() as ctx:
        sb = allocator(nc, ctx)
        norm_h, norm_y = (Norm(sb, name, ctx.enter_context(signals(nc, Norm.names(name)))) for name in ("norm2", "norm3"))
        gain, offset = sb("fi_gain", [P, D]), sb("fi_offset", [P, D])
        y = sb("fi_y", [P, NT, D])
        w_in_rows = sb("fi_w_in_rows", [P, HC, D])
        w_in = sb("fi_w_in", [P, KC, HID])
        w_out = sb("fi_w_out", [P, HC, D])
        bias = sb("fi_bias", [P, HC])
        node = [sb(f"fi_node{b}", [P, D]) for b in range(2)]
        node_t = [sb(f"fi_node_t{b}", [P, KC, P]) for b in range(2)]
        hidden = [sb(f"fi_hidden{b}", [P, HC, P]) for b in range(2)]
        turned = ctx.enter_context(nc.psum_tensor("fi_turned", [P, 2 * BANK], F32))
        hidden_ps = [ctx.enter_context(nc.psum_tensor(f"fi_hidden_ps{b}", [P, BANK], F32)) for b in range(2)]
        out_ps = [ctx.enter_context(nc.psum_tensor(f"fi_out_ps{b}", [P, 2, BANK], F32)) for b in range(2)]
        (affine_loaded, y_loaded, w_loaded, w_turned, w_ready, normed, order, node_ready, turned_done, node_t_ready, hidden_done,
         hidden_ready, out_done, out_taken, stored) = ctx.enter_context(signals(nc, ["fi_" + s for s in (
             "affine_loaded", "y_loaded", "w_loaded", "w_turned", "w_ready", "normed", "order", "node_ready", "turned_done",
             "node_t_ready", "hidden_done", "hidden_ready", "out_done", "out_taken", "stored")]))
        with nc.Block() as block:
            @block.sync
            def _(sp):
                for to, what in ((gain, on_w), (offset, on_b)):
                    sp.dma_start(to[:], what.rearrange("(o n) -> o n", o=1).broadcast_to([P, D])).then_inc(affine_loaded, 16)
                sp.dma_start(y[:].rearrange("p t d -> p (t d)"), x_mix).then_inc(y_loaded, 16)
                sp.dma_start(w_in_rows[:], in_weight.rearrange("(c p) n -> p c n", p=P)).then_inc(w_loaded, 16)
                sp.dma_start(w_out[:], out_weight.rearrange("(c p) n -> p c n", p=P)).then_inc(w_loaded, 16)
                sp.dma_start(bias[:], in_bias.rearrange("(c p) -> p c", p=P), allow_slow_non_contiguous=True).then_inc(w_loaded, 16)
                sp.wait_ge(out_taken, NT + 2)
                sp.dma_start(out[0:FULL * P, :].rearrange("(t p) d -> p t d", p=P), y[:, 0:FULL, :]).then_inc(stored, 16)
                sp.dma_start(out[FULL * P:N, :], y[0:LAST, FULL, :]).then_inc(stored, 16)
                sp.wait_ge(stored, 32)

            @block.scalar
            def _(act):
                for c in range(HC):
                    act.wait_ge(w_turned, c + 1)
                    act.activation(w_in[:, :, c * P:(c + 1) * P], turned[:, 0:D].rearrange("p (c n) -> p c n", c=KC), ACT.Copy).then_inc(w_ready, 1)
                norm_h.scalar(act)
                norm_y.scalar(act)
                act.wait_ge(normed, 1)
                with act.Fori(0, NT // 2) as i:
                    for b in range(2):
                        t = i * 2 + b
                        act.activation(node[b][:], rows_of(nodes, t), ACT.Copy).then_inc(node_ready, 1)
                        act.wait_ge(turned_done, t + 1)
                        act.activation(node_t[b][:], turned[:, 0:D].rearrange("p (c n) -> p c n", c=KC), ACT.Copy).then_inc(node_t_ready, 1)
                        act.wait_ge(hidden_done, t + 1)
                        for c in range(HC):
                            act.activation(hidden[b][:, c, :], hidden_ps[b][:, c * P:(c + 1) * P], ACT.Gelu, bias=bias[:, c:c + 1]).then_inc(hidden_ready, 1)

            @block.tensor
            def _(pe):
                pe.wait_ge(w_loaded, 48)
                for c in range(HC):
                    if c:
                        pe.wait_ge(w_ready, c)
                    for n in range(KC):
                        last = pe.transpose(turned[:, n * P:(n + 1) * P], w_in_rows[:, c, n * P:(n + 1) * P], ident[:])
                    last.then_inc(w_turned, 1)
                pe.wait_ge(w_ready, HC)
                with pe.Fori(0, NT // 2) as i:
                    for b in range(2):
                        t = i * 2 + b
                        pe.wait_ge(node_ready, t + 1)
                        for c in range(KC):
                            last = pe.transpose(turned[:, c * P:(c + 1) * P], node[b][:, c * P:(c + 1) * P], ident[:])
                        last.then_inc(turned_done, 1)
                        pe.wait_ge(node_t_ready, t + 1)
                        for n in range(HC):
                            for c in range(KC):
                                last = pe.matmul(hidden_ps[b][:, n * P:(n + 1) * P], w_in[:, c, n * P:(n + 1) * P], node_t[b][:, c, :],
                                                 start=c == 0, stop=c == KC - 1)
                        last.then_inc(hidden_done, 1)
                        pe.wait_ge(hidden_ready, HC * (t + 1))
                        pe.wait_ge(out_taken, t + 1)
                        for half in range(2):
                            for c in range(HC):
                                last = pe.matmul(out_ps[b][:, half, 0:HALF], hidden[b][:, c, :], w_out[:, c, half * HALF:(half + 1) * HALF],
                                                 start=c == 0, stop=c == HC - 1)
                        last.then_inc(out_done, 1)

            @block.vector
            def _(dve):
                step = Link(dve, order)
                norm_h.vector(dve, nodes)
                dve.wait_ge(affine_loaded, 32)
                step(dve.tensor_tensor(nodes[:], nodes[:], over(gain[:], NT), ALU.mult))
                step(dve.tensor_tensor(nodes[:], nodes[:], over(offset[:], NT), ALU.add))
                dve.wait_ge(y_loaded, 16)
                step(dve.tensor_tensor(y[:], y[:], nodes[:], ALU.add))
                step(dve.tensor_copy(nodes[:], y[:]))
                norm_y.vector(dve, nodes)
                dve.sem_inc(normed, 1)
                dve.sem_inc(out_taken, 2)
                with dve.Fori(0, NT // 2) as i:
                    for b in range(2):
                        t = i * 2 + b
                        dve.wait_ge(out_done, t + 1)
                        row = rows_of(y, t).rearrange("p (s d) -> p s d", s=2)
                        dve.tensor_tensor(row, out_ps[b][:, :, 0:HALF], row, ALU.add).then_inc(out_taken, 1)


def program(nc, x, src, dst, Wsrc, bsrc, Wdst, bdst, attn, ln_w, ln_b, on_w, on_b, W_qkv, b_qkv, W_out, b_out,
            in_weight, in_bias, out_weight, out):
    with ExitStack() as ctx:
        k = persistent(nc, allocator(nc, ctx))
        load_and_norm(x, **k)
        mix(x, W_qkv, b_qkv, W_out, b_out, **k)
        index_edges(src, dst, **k)
        attention_layers(Wsrc, bsrc, Wdst, bdst, attn, ln_w, ln_b, k)
        finish(on_w, on_b, in_weight, in_bias, out_weight, out, **k)


_INS = (['x', 'src', 'dst']
        + ['L0_gnn_' + n for n in ('Wsrc', 'bsrc', 'Wdst', 'bdst', 'attn', 'ln_w', 'ln_b', 'on_w', 'on_b')]
        + ['L0_mix_' + n for n in ('W_qkv', 'b_qkv', 'W_out', 'b_out')]
        + ['L0_ffn_' + n for n in ('in_weight', 'in_bias', 'out_weight')])


def kernel(**inputs):
    import numpy as _np
    import concourse.bacc as _bacc
    from concourse import mybir as _mybir
    from concourse.bass_utils import run_bass_kernel_spmd as _run

    nc = _bacc.Bacc("TRN2", target_bir_lowering=False, num_devices=1)
    arrays, args = {}, []
    for name in _INS:
        a = _np.ascontiguousarray(inputs[name])
        arrays[f"in_{name}"] = a
        args.append(nc.dram_tensor(f"in_{name}", a.shape, _mybir.dt.from_np(a.dtype), kind="ExternalInput").ap())
    out = nc.dram_tensor("out_0", (N, D), F32, kind="ExternalOutput").ap()
    program(nc, *args, out)
    r = _run(nc, [arrays], core_ids=[0])
    return r.results[0]["out_0"]
```

```python
from contextlib import ExitStack, contextmanager

import concourse.bass as bass
from concourse import mybir

F32, BF16, I32 = mybir.dt.float32, mybir.dt.bfloat16, mybir.dt.int32
ALU, ACT, AX = mybir.AluOpType, mybir.ActivationFunctionType, mybir.AxisListType

P = 128
N, D, E = 1250, 768, 41250
LAYERS, H = 2, 8
HD = D // H
NT = -(-N // P)
FULL = N // P
LAST = N - FULL * P
KC = D // P
HALF = D // 2
DX = D + H
HALFX = DX // 2
TC = KC // 2
TH = H // 2
G = 4
ME = G * P
ME_BITS = 9
UNROLL = 4
NG = -(-(E // ME + NT) // UNROLL)
NM = NG * UNROLL
NMX = NM + UNROLL
TG = UNROLL * G
T = NM * G
SPLIT = 3
BANK = 512
FAR = 1e30
TINY = 1e-30
SLOPE = 0.2
LN_EPS = 1e-5
MIX_EPS = 1e-6
MIX_D = 64
PAIRS = D // P
HID = 384
HC = HID // P
EP, ER = 125, E // 125
RAW = -(-E // ME) * ME
assert RAW <= E + ME and EP * ER == E and TC * P == TH * HD and TG * H == P and 2 * MIX_D == P and NMX <= P and 1 << ME_BITS == ME


class Link:

    def __init__(self, engine, sem, at=0):
        self.engine, self.sem, self.at = engine, sem, at

    def __call__(self, instruction):
        self.at = self.at + 1
        instruction.then_inc(self.sem, 1)
        self.engine.wait_ge(self.sem, self.at)


def allocator(nc, ctx):
    def sb(name, shape, dtype=F32):
        return ctx.enter_context(nc.sbuf_tensor(name, shape, dtype))

    return sb


@contextmanager
def signals(nc, names):
    with ExitStack() as ctx:
        sems = [ctx.enter_context(nc.semaphore(name)) for name in names]
        yield sems
        with nc.Block() as block:
            @block.sync
            def _(sp):
                for s in sems:
                    sp.sem_clear(s)


def rows_of(ap, t):
    return ap[:, bass.ds(t, 1), :].rearrange("p o d -> p (o d)")


def over(ap, n):
    return ap.unsqueeze(1).broadcast_to([ap.shape[0], n, ap.shape[1]])


class Norm:

    SIGNALS = ["stats_done", "var_ready", "root_ready", "order", "applied"]

    def __init__(self, sb, name, sems):
        self.stats = sb(name + "_stats", [P, 2 * NT, 6])
        self.mean = sb(name + "_mean", [P, NT])
        self.dev = sb(name + "_dev", [P, NT, 4])
        self.var = sb(name + "_var", [P, NT])
        self.rstd = sb(name + "_rstd", [P, NT])
        self.work = sb(name + "_work", [P, NT])
        self.stats_done, self.var_ready, self.root_ready, self.order, self.applied = sems

    @classmethod
    def names(cls, name):
        return [f"{name}_{s}" for s in cls.SIGNALS]

    def scalar(self, act):
        act.wait_ge(self.var_ready, 1)
        act.activation(self.rstd[:], self.var[:], ACT.Sqrt).then_inc(self.root_ready, 1)

    def vector(self, dve, data):
        step = Link(dve, self.order)
        with dve.Fori(0, NT) as t:
            for half in range(2):
                dve.bn_stats(rows_of(self.stats, t * 2 + half),
                             rows_of(data[:, :, half * HALF:(half + 1) * HALF], t)).then_inc(self.stats_done, 1)
        dve.wait_ge(self.stats_done, 2 * NT)
        groups = self.stats[:].rearrange("p (t h) (e k) -> p t (h e) k", h=2, k=3)
        means, spreads = groups[:, :, :, 1], groups[:, :, :, 2]
        step(dve.tensor_reduce(self.mean[:], means, AX.X, ALU.add))
        step(dve.tensor_scalar(self.mean[:], self.mean[:], 0.25, None, ALU.mult))
        step(dve.tensor_tensor(self.dev[:], means, self.mean[:].unsqueeze(2).broadcast_to([P, NT, 4]), ALU.subtract))
        step(dve.tensor_tensor(self.dev[:], self.dev[:], self.dev[:], ALU.mult))
        step(dve.tensor_reduce(self.var[:], self.dev[:], AX.X, ALU.add))
        step(dve.tensor_reduce(self.work[:], spreads, AX.X, ALU.add))
        step(dve.tensor_scalar(self.var[:], self.var[:], 0.25, LN_EPS, ALU.mult, ALU.add))
        step(dve.scalar_tensor_tensor(self.var[:], self.work[:], 1.0 / D, self.var[:], ALU.mult, ALU.add))
        dve.sem_inc(self.var_ready, 1)
        dve.wait_ge(self.root_ready, 1)
        step(dve.reciprocal(self.rstd[:], self.rstd[:]))
        step(dve.tensor_tensor(self.work[:], self.rstd[:], self.rstd[:], ALU.mult))
        step(dve.tensor_tensor(self.work[:], self.work[:], self.var[:], ALU.mult))
        step(dve.tensor_scalar(self.work[:], self.work[:], -0.5, 1.5, ALU.mult, ALU.add))
        step(dve.tensor_tensor(self.rstd[:], self.rstd[:], self.work[:], ALU.mult))
        with dve.Fori(0, NT) as t:
            dve.tensor_scalar(rows_of(data, t), rows_of(data, t), self.mean[:, bass.ds(t, 1)],
                              self.rstd[:, bass.ds(t, 1)], ALU.subtract, ALU.mult).then_inc(self.applied, 1)
        dve.wait_ge(self.applied, NT)


def load_and_norm(x, nc, nodes, ident, iota_p, iota_row, row_valid, head_mask, **_):
    with ExitStack() as ctx:
        x_loaded, pad_zero, made, *norm_sems = ctx.enter_context(signals(
            nc, ["x_loaded", "pad_zero", "const_made", *Norm.names("norm0")]))
        norm = Norm(allocator(nc, ctx), "norm0", norm_sems)
        with nc.Block() as block:
            @block.sync
            def _(sp):
                sp.dma_start(nodes[:, 0:FULL, :], x[0:FULL * P, :].rearrange("(t p) d -> p t d", p=P)).then_inc(x_loaded, 16)
                sp.wait_ge(pad_zero, 1)
                sp.dma_start(nodes[0:LAST, FULL, :], x[FULL * P:N, :]).then_inc(x_loaded, 16)

            @block.gpsimd
            def _(pool):
                pool.memset(ident[:], 0.0).then_inc(made, 1)
                pool.memset(row_valid[:], 1.0).then_inc(made, 1)
                pool.memset(head_mask[:], 1.0 - SLOPE).then_inc(made, 1)
                pool.wait_ge(made, 3)
                pool.affine_select(out=head_mask[:], in_=head_mask[:], compare_op=ALU.is_ge, fill=0.0, base=0,
                                   pattern=[[P, TC], [-HD, TH]], channel_multiplier=1).then_inc(made, 1)
                pool.wait_ge(made, 4)
                pool.affine_select(out=head_mask[:], in_=head_mask[:], compare_op=ALU.is_ge, fill=0.0, base=HD - 1,
                                   pattern=[[-P, TC], [HD, TH]], channel_multiplier=-1).then_inc(made, 1)
                pool.affine_select(out=ident[:], in_=ident[:], compare_op=ALU.not_equal, fill=1.0, base=0,
                                   pattern=[[-1, P]], channel_multiplier=1).then_inc(made, 1)
                pool.affine_select(out=row_valid[:], in_=row_valid[:], compare_op=ALU.is_ge, fill=0.0, base=N - 1,
                                   pattern=[[-P, NT]], channel_multiplier=-1).then_inc(made, 1)
                pool.iota(iota_p[:], [[0, 1]], base=0, channel_multiplier=1,
                          allow_small_or_imprecise_dtypes=True).then_inc(made, 1)
                pool.iota(iota_row[:], [[1, ME]], base=0, channel_multiplier=0,
                          allow_small_or_imprecise_dtypes=True).then_inc(made, 1)

            @block.scalar
            def _(act):
                norm.scalar(act)

            @block.vector
            def _(dve):
                dve.memset(nodes[:, FULL, :], 0.0).then_inc(pad_zero, 1)
                dve.wait_ge(x_loaded, 32)
                norm.vector(dve, nodes)


def pad_and_check(src, dst, nc, src_pad, dst_pad, unsorted, **_):
    with ExitStack() as ctx:
        sb = allocator(nc, ctx)
        zeros = sb("pc_zeros", [1, ME], I32)
        here_i, next_i = sb("pc_here_i", [EP, ER], I32), sb("pc_next_i", [EP, ER], I32)
        here, after, falls = sb("pc_here", [EP, ER]), sb("pc_after", [EP, ER]), sb("pc_falls", [EP, ER])
        count, ones = sb("pc_count", [EP, 1]), sb("pc_ones", [EP, P])
        ps = ctx.enter_context(nc.psum_tensor("pc_ps", [P, 1], F32))
        made, loaded, padded, order, counted, summed = ctx.enter_context(signals(
            nc, ["pc_" + s for s in ("made", "loaded", "padded", "order", "counted", "summed")]))
        with nc.Block() as block:
            @block.sync
            def _(sp):
                sp.dma_start(here_i[:], dst.rearrange("(p e) -> p e", p=EP)).then_inc(loaded, 16)
                for pad, edges in ((src_pad, src), (dst_pad, dst)):
                    sp.dma_start(pad[0:E].rearrange("(p e) -> p e", p=EP), edges.rearrange("(p e) -> p e", p=EP)).then_inc(padded, 16)
                sp.wait_ge(made, 2)
                sp.dma_start(next_i[0:EP - 1, :], bass.AP(dst.tensor, 1, [[ER, EP - 1], [1, ER]])).then_inc(loaded, 16)
                sp.dma_start(next_i[EP - 1:EP, 0:ER - 1], bass.AP(dst.tensor, E - ER + 1, [[ER, 1], [1, ER - 1]])).then_inc(loaded, 16)
                for pad in (src_pad, dst_pad):
                    sp.dma_start(pad[E:].rearrange("(o e) -> o e", o=1), zeros[:]).then_inc(padded, 16)
                sp.wait_ge(padded, 64)

            @block.gpsimd
            def _(pool):
                pool.memset(zeros[:], 0).then_inc(made, 1)
                pool.memset(next_i[:], N).then_inc(made, 1)

            @block.tensor
            def _(pe):
                pe.wait_ge(counted, 1)
                pe.matmul(ps[:], ones[:], count[:], start=True, stop=True).then_inc(summed, 1)

            @block.vector
            def _(dve):
                step = Link(dve, order)
                step(dve.memset(ones[:], 1.0))
                dve.wait_ge(loaded, 48)
                step(dve.tensor_copy(here[:], here_i[:]))
                step(dve.tensor_copy(after[:], next_i[:]))
                step(dve.tensor_tensor(falls[:], here[:], after[:], ALU.is_gt))
                step(dve.tensor_reduce(count[:], falls[:], AX.X, ALU.add))
                dve.sem_inc(counted, 1)
                dve.wait_ge(summed, 1)
                step(dve.tensor_copy(unsorted[:], ps[0:1, :]))


def sort_edges(src, dst, nc, iota_p, src_pad, dst_pad, unsorted, src_raw, dst_raw, **_):
    C = RAW // ME
    with nc.If(nc.values_load(unsorted[0:1, 0:1], min_val=0, max_val=E) > 0):
        with ExitStack() as ctx:
            sb = allocator(nc, ctx)
            fill = sb("so_fill", [1, RAW - E], I32)
            zeros = sb("so_zeros", [1, RAW - E], I32)
            node = sb("so_node", [P, NT])
            row_i, row, junk = sb("so_row_i", [P, ME], I32), sb("so_row", [P, ME]), sb("so_junk", [P, ME])
            part, below = sb("so_part", [P, NT]), sb("so_below", [P, NT])
            same, upto = sb("so_same", [P, NT, ME]), sb("so_upto", [P, NT, ME])
            none, ones = sb("so_none", [P, ME]), sb("so_ones", [P, 1])
            place = sb("so_place", [P, G], I32)
            ends = [sb(f"so_ends{k}", [P, G], I32) for k in range(2)]
            ps = ctx.enter_context(nc.psum_tensor("so_ps", [P, G], F32))
            made, raw_stored, row_loaded, row_free, order, ready, placed, place_ready, ends_loaded, place_seen = ctx.enter_context(signals(
                nc, ["so_" + s for s in ("made", "raw_stored", "row_loaded", "row_free", "order", "ready", "placed", "place_ready",
                                         "ends_loaded", "place_seen")]))
            scattered = nc.alloc_semaphore("so_scattered")
            COUNT_STEPS, PLACE_STEPS = NT + 2, 5 * NT + 1
            with nc.Block() as block:
                @block.sync
                def _(sp):
                    for raw, edges in ((src_raw, src), (dst_raw, dst)):
                        sp.dma_start(raw[0:E].rearrange("(p e) -> p e", p=EP), edges.rearrange("(p e) -> p e", p=EP)).then_inc(raw_stored, 16)
                    sp.wait_ge(made, 2)
                    for raw, filling in ((src_raw, zeros), (dst_raw, fill)):
                        sp.dma_start(raw[E:].rearrange("(o e) -> o e", o=1), filling[:]).then_inc(raw_stored, 16)
                    sp.wait_ge(raw_stored, 64)
                    destinations = dst_raw.rearrange("(m e) -> m e", e=ME)
                    with sp.Fori(0, C) as c:
                        sp.wait_ge(row_free, c + 1)
                        sp.dma_start(row_i[:], destinations[bass.ds(c, 1), :].broadcast_to([P, ME])).then_inc(row_loaded, 16)
                    with sp.Fori(0, C) as c:
                        sp.wait_ge(row_free, c + (C + 1))
                        sp.dma_start(row_i[:], destinations[bass.ds(c, 1), :].broadcast_to([P, ME])).then_inc(row_loaded, 16)
                        sp.wait_ge(place_seen, c + 1)
                        for raw, to in zip((src_raw, dst_raw), ends):
                            sp.dma_start(to[:], raw[bass.ds(c * ME, ME)].rearrange("(j p) -> p j", p=P),
                                         allow_slow_non_contiguous=True).then_inc(ends_loaded, 16)

                @block.gpsimd
                def _(pool):
                    pool.memset(fill[:], NT * P - 1).then_inc(made, 1)
                    pool.memset(zeros[:], 0).then_inc(made, 1)
                    pool.sem_inc(place_seen, 1)
                    with pool.Fori(0, C) as c:
                        pool.wait_ge(place_ready, c + 2)
                        pool.wait_ge(ends_loaded, c * 32 + 32)
                        pool.sem_inc(made, 1)
                        for pad, what in zip((src_pad, dst_pad), ends):
                            for j in range(G):
                                pool.indirect_dma_start(pad.rearrange("(e o) -> e o", o=1), bass.IndirectOffsetOnAxis(place[:, j:j + 1], 0),
                                                        what[:, j:j + 1], None).then_inc(scattered, 16)
                        pool.wait_ge(scattered, (c + 1) * (2 * G * 16))
                        pool.sem_inc(place_seen, 1)

                @block.scalar
                def _(act):
                    with act.Fori(0, C) as c:
                        act.wait_ge(placed, c + 1)
                        act.wait_ge(place_seen, c + 1)
                        act.activation(place[:], ps[:], ACT.Copy).then_inc(place_ready, 1)

                @block.tensor
                def _(pe):
                    with pe.Fori(0, C) as c:
                        pe.wait_ge(ready, c + 1)
                        pe.wait_ge(place_ready, c + 1)
                        for j in range(G):
                            for t in range(NT):
                                last = pe.matmul(ps[:, j:j + 1], same[:, t, j * P:(j + 1) * P], ones[:], start=t == 0, stop=t == NT - 1)
                        last.then_inc(placed, 1)

                @block.vector
                def _(dve):
                    step = Link(dve, order)
                    for t in range(NT):
                        step(dve.tensor_scalar(node[:, t:t + 1], iota_p[:], float(t * P), None, ALU.add))
                    for what, value in ((none, 0.0), (ones, 1.0), (below, -1.0)):
                        step(dve.memset(what[:], value))
                    dve.sem_inc(row_free, 1)
                    dve.sem_inc(place_ready, 1)
                    at = step.at
                    with dve.Fori(0, C) as c:
                        step = Link(dve, order, c * COUNT_STEPS + at)
                        dve.wait_ge(row_loaded, c * 16 + 16)
                        step(dve.tensor_copy(row[:], row_i[:]))
                        dve.sem_inc(row_free, 1)
                        for t in range(NT):
                            step(dve.tensor_scalar(junk[:], row[:], node[:, t:t + 1], None, ALU.is_lt, ALU.add, accum_out=part[:, t:t + 1]))
                        step(dve.tensor_tensor(below[:], below[:], part[:], ALU.add))
                    at = at + C * COUNT_STEPS
                    with dve.Fori(0, C) as c:
                        step = Link(dve, order, c * PLACE_STEPS + at)
                        dve.wait_ge(row_loaded, c * 16 + (C * 16 + 16))
                        step(dve.tensor_copy(row[:], row_i[:]))
                        dve.sem_inc(row_free, 1)
                        for t in range(NT):
                            step(dve.tensor_scalar(same[:, t, :], row[:], node[:, t:t + 1], None, ALU.is_equal))
                            step(dve.tensor_tensor_scan(upto[:, t, :], none[:], same[:, t, :], 0.0, ALU.add, ALU.add))
                            step(dve.scalar_tensor_tensor(same[:, t, :], upto[:, t, :], below[:, t:t + 1], same[:, t, :], ALU.add, ALU.mult))
                            step(dve.tensor_copy(part[:, t:t + 1], upto[:, t, ME - 1:ME]))
                            step(dve.tensor_tensor(below[:, t:t + 1], below[:, t:t + 1], part[:, t:t + 1], ALU.add))
                        dve.sem_inc(ready, 1)
                        dve.wait_ge(placed, c + 1)


def index_edges(dst, nc, ident, iota_p, iota_row, src_index, dst_local, block_of, new_run, end_run,
                tile_flags, src_pad, dst_pad, local_rows, global_rows, block_list, **_):
    with ExitStack() as ctx:
        sb = allocator(nc, ctx)
        before = sb("ix_before", [1, 1])
        dst_i, dst_f, junk = sb("ix_dst_i", [EP, ER], I32), sb("ix_dst_f", [EP, ER]), sb("ix_junk", [EP, ER])
        count, ones = sb("ix_count", [EP, NT]), sb("ix_ones", [EP, P])
        start = sb("ix_start", [P, NT + 1])
        first = sb("ix_first", [P, NT + 1])
        size, size_i, none = sb("ix_size", [P, NT]), sb("ix_size_i", [P, NT], I32), sb("ix_none", [P, NT])
        passed, step_to, part = sb("ix_passed", [P, NT - 1]), sb("ix_step", [P, NT - 1]), sb("ix_part", [P, NT - 1])
        blk, blk_i, shift = sb("ix_blk", [P, 1]), sb("ix_blk_i", [P, 1], I32), sb("ix_shift", [P, 1])
        base, base_i, valid, end = sb("ix_base", [P, 1]), sb("ix_base_i", [P, 1], I32), sb("ix_valid", [P, 1]), sb("ix_end", [P, 1])
        rows_i = sb("ix_rows_i", [NMX, 2, ME], I32)
        rows = sb("ix_rows", [NMX, 2, ME])
        mask, glob, local = sb("ix_mask", [NMX, ME]), sb("ix_glob", [NMX, ME]), sb("ix_local", [NMX, ME])
        local_b = sb("ix_local_b", [NMX, ME], BF16)
        around = sb("ix_around", [P, NG, P + 2])
        edge_of = sb("ix_edge_of", [H, 4, T])
        ps = ctx.enter_context(nc.psum_tensor("ix_ps", [P, 3, BANK], F32))
        (order, before_made, dst_loaded, counted, summed, base_made, lists_made, stored, listed,
         cols_ready, flags_loaded) = ctx.enter_context(signals(nc, ["ix_" + s for s in (
             "order", "before_made", "dst_loaded", "counted", "summed", "base_made",
             "lists_made", "stored", "listed", "cols_ready", "flags_loaded")]))
        gathered = nc.alloc_semaphore("ix_gathered")
        with nc.Block() as block:
            @block.sync
            def _(sp):
                sp.dma_start(dst_i[:], dst.rearrange("(p e) -> p e", p=EP)).then_inc(dst_loaded, 16)
                sp.wait_ge(before_made, 1)
                sp.dma_start(global_rows[0:1].rearrange("(o e) -> o e", o=1), before[:]).then_inc(stored, 16)
                sp.wait_ge(lists_made, 3)
                sp.dma_start(global_rows[1:1 + NMX * ME].rearrange("(m e) -> m e", m=NMX), glob[:]).then_inc(stored, 16)
                sp.dma_start(local_rows, local_b[:]).then_inc(stored, 16)
                sp.dma_start(block_list.rearrange("(m o) -> m o", o=1), blk_i[0:NMX, :]).then_inc(stored, 16)
                sp.wait_ge(stored, 64)
                sp.dma_start(block_of[:], block_list.rearrange("(o m) -> o m", o=1)).then_inc(listed, 16)
                for h in range(H):
                    sp.dma_start(around[h * TG:(h + 1) * TG], bass.AP(
                        global_rows.tensor, 0, [[P, TG], [TG * P, NG], [1, P + 2]])).then_inc(flags_loaded, 16)
                for k, at in enumerate((0, 1, P, P + 1)):
                    sp.dma_start(edge_of[:, k, :], bass.AP(global_rows.tensor, at, [[0, H], [P, T]]), allow_slow_non_contiguous=True).then_inc(flags_loaded, 16)
                sp.wait_ge(listed, 16)

            @block.gpsimd
            def _(pool):
                pool.memset(before[:], -2.0).then_inc(before_made, 1)
                pool.wait_ge(base_made, 1)
                for k, pad in enumerate((src_pad, dst_pad)):
                    pool.indirect_dma_start(rows_i[:, k, :], None, pad.rearrange("(e o) -> e o", o=1),
                                            bass.IndirectOffsetOnAxis(base_i[0:NMX, 0:1], 0)).then_inc(gathered, 16)

            @block.tensor
            def _(pe):
                pe.wait_ge(counted, 1)
                pe.matmul(ps[:, 0, 0:NT], ones[:], count[:], start=True, stop=True).then_inc(summed, 1)
                pe.wait_ge(cols_ready, 2)
                for k, what in enumerate((rows[:, 0, :], local[:])):
                    for j in range(G):
                        pe.transpose(ps[:, 1 + k, j * P:j * P + NMX], what[:, j * P:(j + 1) * P],
                                     ident[0:NMX, 0:NMX]).then_inc(summed, 1)

            @block.vector
            def _(dve):
                step = Link(dve, order)
                dve.memset(ones[:], 1.0).then_inc(order, 1)
                dve.memset(none[:], 0.0).then_inc(order, 1)
                dve.memset(start[:, 0:1], 0.0).then_inc(order, 1)
                dve.memset(first[:, 0:1], 0.0).then_inc(order, 1)
                step.at = 4
                dve.wait_ge(dst_loaded, 16)
                step(dve.tensor_copy(dst_f[:], dst_i[:]))
                for b in range(NT):
                    step(dve.tensor_scalar(junk[:], dst_f[:], float((b + 1) * P), None, ALU.is_lt, ALU.add,
                                           accum_out=count[:, b:b + 1]))
                dve.sem_inc(counted, 1)
                dve.wait_ge(summed, 1)
                step(dve.tensor_copy(start[:, 1:], ps[:, 0, 0:NT]))
                step(dve.tensor_tensor(size[:], start[:, 1:], start[:, 0:NT], ALU.subtract))
                step(dve.tensor_scalar(size[:], size[:], float(ME - 1), None, ALU.add))
                step(dve.tensor_copy(size_i[:], size[:]))
                step(dve.tensor_scalar(size_i[:], size_i[:], ME_BITS, None, ALU.arith_shift_right))
                step(dve.tensor_copy(size[:], size_i[:]))
                step(dve.tensor_tensor_scan(first[:, 1:], none[:], size[:], 0.0, ALU.add, ALU.add))
                step(dve.tensor_scalar(passed[:], first[:, 1:NT], iota_p[:], None, ALU.is_le))
                step(dve.tensor_reduce(blk[:], passed[:], AX.X, ALU.add))
                step(dve.tensor_tensor(step_to[:], first[:, 1:NT], first[:, 0:NT - 1], ALU.subtract))
                step(dve.tensor_scalar(step_to[:], step_to[:], float(-ME), None, ALU.mult))
                step(dve.tensor_tensor(step_to[:], step_to[:], start[:, 1:NT], ALU.add))
                step(dve.tensor_tensor(step_to[:], step_to[:], start[:, 0:NT - 1], ALU.subtract))
                step(dve.tensor_tensor(part[:], passed[:], step_to[:], ALU.mult))
                step(dve.tensor_reduce(base[:], part[:], AX.X, ALU.add))
                step(dve.tensor_scalar(shift[:], iota_p[:], float(ME), None, ALU.mult))
                step(dve.tensor_tensor(base[:], base[:], shift[:], ALU.add))
                step(dve.tensor_scalar(base[:], base[:], float(E), None, ALU.min))
                step(dve.tensor_copy(base_i[:], base[:]))
                dve.sem_inc(base_made, 1)
                step(dve.tensor_tensor(step_to[:], start[:, 2:], start[:, 1:NT], ALU.subtract))
                step(dve.tensor_tensor(part[:], passed[:], step_to[:], ALU.mult))
                step(dve.tensor_reduce(end[:], part[:], AX.X, ALU.add))
                step(dve.tensor_tensor(end[:], end[:], start[:, 1:2], ALU.add))
                step(dve.tensor_tensor(valid[:], end[:], base[:], ALU.subtract))
                step(dve.tensor_copy(blk_i[:], blk[:]))
                dve.sem_inc(lists_made, 1)
                step(dve.tensor_scalar(shift[:], blk[:], float(-P), 1.0, ALU.mult, ALU.add))
                step(dve.tensor_scalar(mask[:], iota_row[0:NMX], valid[0:NMX], None, ALU.is_lt))
                dve.wait_ge(gathered, 32)
                step(dve.tensor_copy(rows[:], rows_i[:]))
                step(dve.tensor_tensor(rows[:, 0, :], rows[:, 0, :], mask[:], ALU.mult))
                step(dve.scalar_tensor_tensor(glob[:], rows[:, 1, :], 1.0, mask[:], ALU.add, ALU.mult))
                step(dve.tensor_scalar(glob[:], glob[:], -1.0, None, ALU.add))
                dve.sem_inc(lists_made, 1)
                step(dve.scalar_tensor_tensor(local[:], rows[:, 1, :], shift[0:NMX], mask[:], ALU.add, ALU.mult))
                step(dve.tensor_scalar(local[:], local[:], -1.0, None, ALU.add))
                dve.sem_inc(cols_ready, 2)
                step(dve.tensor_copy(local_b[:], local[:]))
                dve.sem_inc(lists_made, 1)
                dve.wait_ge(summed, 1 + 2 * G)
                for k, columns in enumerate((src_index, dst_local)):
                    step(dve.tensor_copy(columns[:].rearrange("p m j -> p j m"),
                                         ps[:, 1 + k, :].rearrange("p (j m) -> p j m", j=G)[:, :, 0:NMX]))
                dve.wait_ge(flags_loaded, 16 * (H + 4))
                for flags, beside, alone in ((new_run, 0, 0), (end_run, 2, P - 1)):
                    step(dve.tensor_tensor(flags[:], around[:, :, 1:P + 1], around[:, :, beside:P + beside], ALU.not_equal))
                    step(dve.tensor_scalar(flags[:], flags[:], -FAR, None, ALU.mult))
                    step(dve.memset(flags[:, :, alone:alone + 1], -FAR))
                for k, (a, b) in enumerate(((0, 2), (0, 1), (1, 3), (2, 3))):
                    step(dve.tensor_tensor(tile_flags[:, k, :], edge_of[:, a, :], edge_of[:, b, :], ALU.not_equal))
                step(dve.tensor_scalar(tile_flags[:], tile_flags[:], -FAR, None, ALU.mult))


def persistent(nc, sb):
    def dram(name, shape, dtype=F32):
        return nc.dram_tensor(name, shape, dtype).ap()

    return dict(
        nc=nc,
        ident=sb("ident", [P, P]),
        iota_p=sb("iota_p", [P, 1]),
        iota_row=sb("iota_row", [P, ME]),
        nodes=sb("nodes", [P, NT, D]),
        head_mask=sb("head_mask", [P, TC, TH]),
        row_valid=sb("row_valid", [P, NT]),
        src_index=sb("src_index", [P, NMX, G], I32),
        dst_local=sb("dst_local", [P, NMX, G]),
        block_of=sb("block_of", [1, NMX], I32),
        new_run=sb("new_run", [P, NG, P]),
        end_run=sb("end_run", [P, NG, P]),
        tile_flags=sb("tile_flags", [H, 4, T]),
        unsorted=sb("unsorted", [1, 1], I32),
        src_raw=dram("src_raw", [RAW], I32),
        dst_raw=dram("dst_raw", [RAW], I32),
        src_pad=dram("src_pad", [E + ME], I32),
        dst_pad=dram("dst_pad", [E + ME], I32),
        local_rows=dram("local_rows", [NMX, ME], BF16),
        global_rows=dram("global_rows", [1 + NMX * ME]),
        block_list=dram("block_list", [NMX], I32),
        table=dram("table", [NT * P, DX]),
        x_mix=dram("x_mix", [P, NT * D]),
        tails=dram("tails", [2, NG, H, TG]),
        carries=dram("carries", [2, NG, H, TG]),
    )


def project(layer, Wsrc, bsrc, Wdst, bdst, attn, attn_relu, dst_rows, sems, nc, ident, nodes, table, **_):
    with ExitStack() as ctx:
        sb = allocator(nc, ctx)
        weights = [sb(f"pr_w{s}", [P, KC, D]) for s in range(2)]
        bias = [sb(f"pr_b{s}", [P, D]) for s in range(2)]
        attn_lin = sb("pr_attn_lin", [P, D])
        node = [sb(f"pr_node{b}", [P, D]) for b in range(2)]
        node_t = [sb(f"pr_node_t{b}", [P, KC, P]) for b in range(2)]
        src_row = [sb(f"pr_src_row{b}", [P, DX]) for b in range(2)]
        dst_row = sb("pr_dst_row", [P, DX])
        rest = sb("pr_rest", [P, DX])
        prod = sb("pr_prod", [P, D])
        turned = ctx.enter_context(nc.psum_tensor("pr_turned", [P, 2 * BANK], F32))
        src_ps = ctx.enter_context(nc.psum_tensor("pr_src_ps", [P, 2, BANK], F32))
        dst_ps = ctx.enter_context(nc.psum_tensor("pr_dst_ps", [P, 2, BANK], F32))
        (src_w_loaded, dst_w_loaded, bias_loaded, attn_loaded, attn_ready, node_ready, turned_done, node_t_ready, src_done, dst_done, src_taken,
         dst_taken, row_ready, row_stored, row_free, order, split_ready, split_done, node_t_free) = names = [nc.alloc_semaphore("pr_" + s) for s in (
             "src_w_loaded", "dst_w_loaded", "bias_loaded", "attn_loaded", "attn_ready", "node_ready", "turned_done", "node_t_ready", "src_done", "dst_done",
             "src_taken", "dst_taken", "row_ready", "row_stored", "row_free", "order", "split_ready", "split_done", "node_t_free")]
        sems += names
        STEPS = 8
        with nc.Block() as block:
            @block.sync
            def _(sp):
                sp.dma_start(attn_lin[:], attn.rearrange("l h d -> l (h d)")[bass.ds(layer, 1), :].broadcast_to([P, D])).then_inc(attn_loaded, 16)
                for s, b in enumerate((bsrc, bdst)):
                    sp.dma_start(bias[s][:], b[bass.ds(layer, 1), :].broadcast_to([P, D])).then_inc(bias_loaded, 16)
                for s, (w, loaded) in enumerate(((Wsrc, src_w_loaded), (Wdst, dst_w_loaded))):
                    sp.dma_start(weights[s][:], w.rearrange("l k n -> (l k) n")[bass.ds(layer * D, D), :]
                                 .rearrange("(c p) n -> p c n", p=P)).then_inc(loaded, 16)
                with sp.Fori(0, NT // 2) as i:
                    for b in range(2):
                        t = i * 2 + b
                        sp.wait_ge(row_ready, t + 1)
                        sp.dma_start(table[bass.ds(t * P, P), :], src_row[b][:]).then_inc(row_stored, 16)
                        sp.wait_ge(row_stored, 16 * t + 16)
                        sp.sem_inc(row_free, 1)

            @block.scalar
            def _(act):
                act.wait_ge(attn_loaded, 16)
                act.activation(attn_relu[:], attn_lin[:], ACT.Copy, scale=1.0 - SLOPE).then_inc(attn_ready, 1)
                act.wait_ge(attn_ready, 1)
                act.activation(attn_lin[:], attn_lin[:], ACT.Copy, scale=SLOPE).then_inc(attn_ready, 1)

                def copy_node(t, b):
                    act.activation(node[b][:], rows_of(nodes, t), ACT.Copy).then_inc(node_ready, 1)

                def copy_turned(t, b):
                    act.wait_ge(turned_done, t + 1)
                    act.wait_ge(node_t_free, t + 1)
                    act.activation(node_t[b][:], turned[:, 0:D].rearrange("p (c n) -> p c n", c=KC), ACT.Copy).then_inc(node_t_ready, 1)

                def split(t):
                    for s, what in enumerate((dst_row, rest, rest)):
                        act.wait_ge(split_ready, SPLIT * t + s + 1)
                        act.activation(dst_rows[:, bass.ds(t, 1), s, :].rearrange("p o d -> p (o d)"), what[:], ACT.Copy).then_inc(split_done, 1)

                copy_node(0, 0)
                copy_turned(0, 0)
                copy_node(1, 1)
                with act.Fori(0, NT // 2 - 1) as i:
                    for b in range(2):
                        t = i * 2 + b
                        copy_turned(t + 1, 1 - b)
                        copy_node(t + 2, b)
                        split(t)
                copy_turned(NT - 1, 1)
                split(NT - 2)
                split(NT - 1)

            @block.tensor
            def _(pe):

                def turn(t, b):
                    pe.wait_ge(node_ready, t + 1)
                    pe.wait_ge(node_t_ready, t + 1)
                    for c in range(KC):
                        last = pe.transpose(turned[:, c * P:(c + 1) * P], node[b][:, c * P:(c + 1) * P], ident[:])
                    last.then_inc(turned_done, 1)

                def product(t, b, w, loaded, ps, taken, done):
                    pe.wait_ge(loaded, 16)
                    pe.wait_ge(taken, t + 1)
                    for half in range(2):
                        for c in range(KC):
                            last = pe.matmul(ps[:, half, 0:HALF], node_t[b][:, c, :],
                                             w[:, c, half * HALF:(half + 1) * HALF], start=c == 0, stop=c == KC - 1)
                    last.then_inc(done, 1)

                def tile(t, b, more=True):
                    pe.wait_ge(node_t_ready, t + 2)
                    product(t, b, weights[0], src_w_loaded, src_ps, src_taken, src_done)
                    if more:
                        turn(t + 1, 1 - b)
                    product(t, b, weights[1], dst_w_loaded, dst_ps, dst_taken, dst_done)
                    pe.wait_ge(dst_done, t + 1)
                    pe.sem_inc(node_t_free, 1)

                pe.sem_inc(node_t_ready, 1)
                pe.sem_inc(node_t_free, 2)
                turn(0, 0)
                with pe.Fori(0, NT // 2 - 1) as i:
                    for b in range(2):
                        tile(i * 2 + b, b)
                tile(NT - 2, 0)
                tile(NT - 1, 1, more=False)

            @block.vector
            def _(dve):
                dve.sem_inc(src_taken, 1)
                dve.sem_inc(dst_taken, 1)
                dve.sem_inc(row_free, 2)
                dve.wait_ge(bias_loaded, 32)
                dve.wait_ge(attn_ready, 2)
                with dve.Fori(0, NT // 2) as i:
                    for b in range(2):
                        t = i * 2 + b
                        step = Link(dve, order, t * STEPS)
                        dve.wait_ge(row_free, t + 1)
                        for row, ps, offset, taken, done in ((src_row[b], src_ps, bias[0], src_taken, src_done),
                                                             (dst_row, dst_ps, bias[1], dst_taken, dst_done)):
                            dve.wait_ge(done, t + 1)
                            step(dve.tensor_tensor(row[:, 0:D].rearrange("p (s d) -> p s d", s=2), ps[:, :, 0:HALF],
                                                   offset[:].rearrange("p (s d) -> p s d", s=2), ALU.add))
                            dve.sem_inc(taken, 1)
                            step(dve.tensor_tensor(prod[:], row[:, 0:D], attn_lin[:], ALU.mult))
                            step(dve.tensor_reduce(row[:, D:DX], prod[:].rearrange("p (h d) -> p h d", h=H), AX.X, ALU.add))
                            if row is dst_row:
                                dve.sem_inc(split_ready, 1)
                            else:
                                dve.sem_inc(row_ready, 1)
                        whole = dst_row
                        for s in range(SPLIT - 1):
                            dve.wait_ge(split_done, 3 * t + s + 1)
                            step(dve.tensor_tensor(rest[:], whole[:], dst_rows[:, bass.ds(t, 1), s, :].rearrange("p o d -> p (o d)"), ALU.subtract))
                            dve.sem_inc(split_ready, 1)
                            whole = rest
                        dve.wait_ge(split_done, 3 * t + 3)


AHEAD = 2


def landed(layer, b, rounds):
    return 16 * G * (layer * (NG + (b < AHEAD)) + rounds)


def logits_of_edges(layer, table, attn, local_rows, src_index, block_of, iota_p, ident, head_mask, attn_relu, dst_rows, logits,
                    sems, nc, **_):
    with ExitStack() as ctx:
        sb = allocator(nc, ctx)
        rows = [sb(f"lg_rows{b}", [P, G, DX]) for b in range(UNROLL)]
        index = [sb(f"lg_index{b}", [P, G], I32) for b in range(UNROLL)]
        local = [sb(f"lg_local{b}", [P, ME], BF16) for b in range(UNROLL)]
        place = [sb(f"lg_place{b}", [P, ME], BF16) for b in range(UNROLL)]
        relu = [sb(f"lg_relu{b}", [P, TC, ME]) for b in range(2)]
        attn_col = sb("lg_attn_col", [P, TC])
        attn_diag = sb("lg_attn_diag", [P, TC, TH])
        turned = [ctx.enter_context(nc.psum_tensor(f"lg_turned{c}", [P, BANK], F32)) for c in range(TC)]
        ends = [ctx.enter_context(nc.psum_tensor(f"lg_ends{j}", [P, BANK], F32)) for j in range(G)]
        products = ctx.enter_context(nc.psum_tensor("lg_products", [P, G, TH], F32))
        (index_ready, index_seen, local_free, place_ready, turned_done, turned_relu, products_done, products_taken, ends_done, ends_free,
         added, rows_free, relu_done, pool_done, dve_done, reduced, attn_loaded, attn_ready) = names = [nc.alloc_semaphore("lg_" + s) for s in (
             "index_ready", "index_seen", "local_free", "place_ready", "turned_done", "turned_relu", "products_done", "products_taken",
             "ends_done", "ends_free", "added", "rows_free", "relu_done", "pool_done", "dve_done", "reduced", "attn_loaded", "attn_ready")]
        gathered = [nc.alloc_semaphore(f"lg_gathered{b}") for b in range(UNROLL)]
        local_loaded = [nc.alloc_semaphore(f"lg_local_loaded{b}") for b in range(UNROLL)]
        sems += [*names, *local_loaded]
        POOL = 2
        with nc.Block() as block:
            @block.sync
            def _(sp):
                sp.dma_start(attn_col[:], attn.rearrange("l h d -> (l h d)")[bass.ds(layer * D, HALF)].rearrange("(c p) -> p c", p=P),
                             allow_slow_non_contiguous=True).then_inc(attn_loaded, 16)

                def load_local(m, b):
                    sp.wait_ge(local_free, m + 1)
                    sp.dma_start(local[b][:], local_rows[bass.ds(m, 1), :].broadcast_to([P, ME])).then_inc(local_loaded[b], 16)

                with sp.Fori(0, NG) as i:
                    for b in range(UNROLL):
                        load_local(i * UNROLL + b, b)
                for b in range(AHEAD):
                    load_local(NM + b, b)
                for b in range(UNROLL):
                    sp.wait_ge(local_loaded[b], 16 * (NG + (b < AHEAD)))

            @block.gpsimd
            def _(pool):
                def gather(m, b):
                    pool.wait_ge(rows_free, m + 1)
                    pool.tensor_copy(index[b][:], rows_of(src_index, m)).then_inc(index_ready, 1)
                    pool.wait_ge(index_ready, m + 1)
                    pool.sem_inc(index_seen, 1)
                    for j in range(G):
                        pool.indirect_dma_start(rows[b][:, j, :], None, table,
                                                bass.IndirectOffsetOnAxis(index[b][:, j:j + 1], 0)).then_inc(gathered[b], 16)

                for m in range(AHEAD):
                    gather(m, m)
                with pool.Fori(0, NG) as i:
                    for b in range(UNROLL):
                        m = i * UNROLL + b
                        gather(m + AHEAD, (b + AHEAD) % UNROLL)
                        pool.wait_ge(relu_done, m + 1)
                        pool.tensor_tensor(rows[b][:, 0:POOL, HALF:D], rows[b][:, 0:POOL, HALF:D], over(attn_relu[:, HALF:], POOL),
                                           ALU.mult).then_inc(pool_done, 1)
                for b in range(UNROLL):
                    pool.wait_ge(gathered[b], landed(layer, b, NG + (b < AHEAD)))

            @block.scalar
            def _(act):
                act.sem_inc(turned_relu, TC)
                with act.Fori(0, NG) as i:
                    for b in range(UNROLL):
                        m = i * UNROLL + b
                        act.wait_ge(products_done, m + 1)
                        for c in range(TC):
                            act.wait_ge(turned_done, m * TC + c + 1)
                            act.activation(relu[b % 2][:, c, :], turned[c][:], ACT.Relu).then_inc(turned_relu, 1)
                        act.wait_ge(added, G * m + POOL)
                        act.activation(rows[b][:, 0:POOL, HALF:D], rows[b][:, 0:POOL, HALF:D], ACT.Relu).then_inc(relu_done, 1)

            @block.tensor
            def _(pe):
                def part(block_at, s, at, n):
                    return dst_rows[:, bass.ds(block_at, 1), s, at:at + n].rearrange("p o d -> p (o d)")

                def turn(m, b, round, block_at):
                    pe.wait_ge(gathered[b], landed(layer, b, round + 1))
                    pe.wait_ge(place_ready, m + 1)
                    for c in range(TC):
                        pe.wait_ge(turned_relu, m * TC + c + 1)
                        for s in range(SPLIT):
                            pe.matmul(turned[c][:], part(block_at, s, c * P, P), place[b][:], start=s == 0, stop=False)
                        for j in range(G):
                            last = pe.matmul(turned[c][:, j * P:(j + 1) * P], rows[b][:, j, c * P:(c + 1) * P], ident[:],
                                             is_transpose=True, start=False, stop=j == G - 1)
                        last.then_inc(turned_done, 1)

                def sum_with_attn(m, b):
                    pe.wait_ge(turned_relu, (m + 2) * TC)
                    pe.wait_ge(products_taken, m + 1)
                    for j in range(G):
                        for c in range(TC):
                            last = pe.matmul(products[:, j, :], relu[b % 2][:, c, j * P:(j + 1) * P], attn_diag[:, c, :],
                                             start=c == 0, stop=c == TC - 1)
                    last.then_inc(products_done, 1)

                def ends_of(m, b, block_at):
                    for j in range(G):
                        pe.wait_ge(ends_free, m * G + j + 1)
                        for s in range(SPLIT):
                            last = pe.matmul(ends[j][:, 0:DX - HALF], place[b][:, j * P:(j + 1) * P], part(block_at, s, HALF, DX - HALF),
                                             start=s == 0, stop=s == SPLIT - 1)
                        last.then_inc(ends_done, 1)

                def block_at(m):
                    return pe.value_load(block_of[0:1, bass.ds(m, 1)], min_val=0, max_val=NT - 1)

                pe.sem_inc(products_done, 2)
                pe.wait_ge(attn_ready, 1)
                first = block_at(0)
                turn(0, 0, 0, first)
                ends_of(0, 0, first)
                with pe.Fori(0, NG) as i:
                    for b in range(UNROLL):
                        m = i * UNROLL + b
                        n = (b + 1) % UNROLL
                        at = block_at(m + 1)
                        turn(m + 1, n, i + (b + 1) // UNROLL, at)
                        sum_with_attn(m, b)
                        ends_of(m + 1, n, at)

            @block.vector
            def _(dve):
                def build_place(m, b, round):
                    dve.wait_ge(local_loaded[b], 16 * (round + 1))
                    dve.tensor_scalar(place[b][:], local[b][:], iota_p[:], None, ALU.is_equal).then_inc(place_ready, 1)
                    dve.wait_ge(place_ready, m + 1)
                    dve.sem_inc(local_free, 1)

                def add_ends(m, b, round):
                    dve.wait_ge(gathered[b], landed(layer, b, round + 1))
                    for j in range(G):
                        dve.wait_ge(ends_done, m * G + j + 1)
                        row = rows[b][:, j, HALF:DX]
                        dve.tensor_tensor(row, ends[j][:, 0:DX - HALF], row, ALU.add).then_inc(added, 1)
                    dve.wait_ge(added, m * G + G)
                    dve.sem_inc(ends_free, G)
                    dve.scalar_tensor_tensor(rows[b][:, POOL:, HALF:D], rows[b][:, POOL:, HALF:D], 0.0, over(attn_relu[:, HALF:], G - POOL),
                                             ALU.max, ALU.mult).then_inc(dve_done, 1)

                def reduce(m, i, b):
                    out = logits[:, bass.ds(i, 1), :, b * G:(b + 1) * G].rearrange("p o h j -> p j (o h)")
                    dve.wait_ge(products_done, m + 3)
                    dve.tensor_tensor(out[:, :, 0:TH], products[:], rows[b][:, :, D:D + TH], ALU.add).then_inc(products_taken, 1)
                    dve.wait_ge(dve_done, m + 1)
                    dve.wait_ge(pool_done, m + 1)
                    dve.tensor_reduce(out[:, :, TH:], rows[b][:, :, HALF:D].rearrange("p j (h d) -> p j h d", d=HD), AX.X, ALU.add).then_inc(reduced, 1)
                    dve.wait_ge(reduced, 2 * m + 1)
                    dve.tensor_tensor(out[:, :, TH:], out[:, :, TH:], rows[b][:, :, D + TH:DX], ALU.add).then_inc(reduced, 1)
                    dve.wait_ge(products_taken, m + 2)
                    dve.wait_ge(reduced, 2 * m + 2)
                    dve.sem_inc(rows_free, 1)

                dve.wait_ge(attn_loaded, 16)
                dve.tensor_tensor(attn_diag[:], head_mask[:], attn_col[:].unsqueeze(2).broadcast_to([P, TC, TH]), ALU.mult).then_inc(attn_ready, 1)
                dve.sem_inc(local_free, UNROLL)
                dve.sem_inc(rows_free, UNROLL)
                dve.sem_inc(ends_free, G)
                dve.sem_inc(products_taken, 1)
                build_place(0, 0, 0)
                build_place(1, 1, 0)
                add_ends(0, 0, 0)
                with dve.Fori(0, NG) as i:
                    for b in range(UNROLL):
                        m = i * UNROLL + b
                        build_place(m + 2, (b + 2) % UNROLL, i + (b + 2) // UNROLL)
                        reduce(m, i, b)
                        add_ends(m + 1, (b + 1) % UNROLL, i + (b + 1) // UNROLL)
                dve.wait_ge(dve_done, NM + 1)


def softmax_weights(logits, ident, new_run, end_run, tile_flags, tails, carries, sems, nc, **_):
    with ExitStack() as ctx:
        sb = allocator(nc, ctx)
        turned, left, right = sb("sm_turned", [P, NG, P]), sb("sm_left", [P, NG, P]), sb("sm_right", [P, NG, P])
        tail, kept = sb("sm_tail", [P, 2, NG]), sb("sm_kept", [P, 2, NG])
        tail_t, carry_t = sb("sm_tail_t", [2 * NG, P]), sb("sm_carry_t", [2 * NG, P])
        runs = sb("sm_runs", [H, 2, T])
        through = sb("sm_through", [H, 2, T])
        carry = sb("sm_carry", [H, 2, T])
        QUADS = -(-NG // 4)
        ps = ctx.enter_context(nc.psum_tensor("sm_ps", [P, QUADS, BANK], F32))
        ps_tail = ctx.enter_context(nc.psum_tensor("sm_ps_tail", [P, BANK], F32))
        ps_carry = ctx.enter_context(nc.psum_tensor("sm_ps_carry", [P, BANK], F32))
        (filled, taken, tails_ready, tail_done, tail_ready, tails_moved, runs_ready, carry_ready, carry_stored, carries_moved,
         carry_done, shifted, exps, back, order, written) = names = [nc.alloc_semaphore("sm_" + s) for s in (
             "filled", "taken", "tails_ready", "tail_done", "tail_ready", "tails_moved", "runs_ready", "carry_ready", "carry_stored",
             "carries_moved", "carry_done", "shifted", "exps", "back", "order", "written")]
        sems += names

        def flat(ap):
            return ap.rearrange("p g e -> p (g e)")

        def quad(ap, q):
            n = min(4, NG - 4 * q)
            return ap[:, 4 * q:4 * q + n], n * P

        with nc.Block() as block:
            @block.tensor
            def _(pe):
                for g in range(NG):
                    last = pe.transpose(ps[:, g // 4, g % 4 * P:(g % 4 + 1) * P], logits[:, g].rearrange("p h t -> p (h t)"), ident[:])
                    if g % 4 == 3 or g == NG - 1:
                        last.then_inc(filled, 1)
                pe.wait_ge(tails_ready, 1)
                pe.transpose(ps_tail[0:2 * NG, 0:P], tail[:].rearrange("p k g -> p (k g)"), ident[:]).then_inc(tail_done, 1)
                pe.wait_ge(carries_moved, 16)
                pe.transpose(ps_carry[:, 0:2 * NG], carry_t[:], ident[0:2 * NG, 0:2 * NG]).then_inc(carry_done, 1)
                for g in range(NG):
                    if g % 4 == 0:
                        pe.wait_ge(exps, g // 4 + 1)
                    last = pe.transpose(ps[:, g // 4, g % 4 * P:(g % 4 + 1) * P], turned[:, g, :], ident[:])
                    if g % 4 == 3 or g == NG - 1:
                        last.then_inc(back, 1)

            @block.scalar
            def _(act):
                for q in range(QUADS):
                    act.wait_ge(filled, q + 1)
                    to, n = quad(turned, q)
                    act.activation(flat(to), ps[:, q, 0:n], ACT.Copy).then_inc(taken, 1)
                act.wait_ge(tail_done, 1)
                act.activation(tail_t[:], ps_tail[0:2 * NG, 0:P], ACT.Copy).then_inc(tail_ready, 1)
                for q in range(QUADS):
                    if q == 0:
                        act.wait_ge(shifted, 1)
                    to, n = quad(turned, q)
                    act.activation(flat(to), flat(to), ACT.Exp).then_inc(exps, 1)
                for q in range(QUADS):
                    act.wait_ge(back, q + 1)
                    to, n = quad(logits, q)
                    act.activation(to.rearrange("p g h t -> p (g h t)"), ps[:, q, 0:n], ACT.Copy).then_inc(written, 1)

            @block.sync
            def _(sp):
                sp.wait_ge(tail_ready, 1)
                sp.dma_start(tails.rearrange("k g h t -> (k g) (h t)"), tail_t[:]).then_inc(tails_moved, 16)
                sp.wait_ge(tails_moved, 16)
                for k in range(2):
                    sp.dma_start(runs[:, k, :].rearrange("h (g t) -> h g t", t=TG), tails[k].rearrange("g h t -> h g t")).then_inc(runs_ready, 16)
                sp.wait_ge(carry_ready, 1)
                for k in range(2):
                    sp.dma_start(carries[k].rearrange("g h t -> h g t"), carry[:, k, :].rearrange("h (g t) -> h g t", t=TG)).then_inc(carry_stored, 16)
                sp.wait_ge(carry_stored, 32)
                sp.dma_start(carry_t[:], carries.rearrange("k g h t -> (k g) (h t)")).then_inc(carries_moved, 16)
                sp.wait_ge(carries_moved, 16)

            @block.vector
            def _(dve):
                step = Link(dve, order)

                def running():
                    step(dve.tensor_tensor_scan(flat(left[:]), flat(new_run[:]), flat(turned[:]), -FAR, ALU.add, ALU.max))
                    step(dve.tensor_tensor_scan(flat(right[:])[:, ::-1], flat(end_run[:])[:, ::-1], flat(turned[:])[:, ::-1],
                                                -FAR, ALU.add, ALU.max))

                dve.wait_ge(taken, QUADS)
                running()
                step(dve.tensor_copy(tail[:, 0, :], left[:, :, P - 1]))
                step(dve.tensor_copy(tail[:, 1, :], right[:, :, 0]))
                dve.sem_inc(tails_ready, 1)
                step(dve.tensor_copy(kept[:, 0, :], turned[:, :, 0]))
                step(dve.tensor_copy(kept[:, 1, :], turned[:, :, P - 1]))
                dve.wait_ge(runs_ready, 32)
                step(dve.tensor_tensor_scan(through[:, 0, :], tile_flags[:, 0, :], runs[:, 0, :], -FAR, ALU.add, ALU.max))
                step(dve.tensor_tensor_scan(through[:, 1, ::-1], tile_flags[:, 2, ::-1], runs[:, 1, ::-1], -FAR, ALU.add, ALU.max))
                step(dve.memset(carry[:, 0, 0:1], -FAR))
                step(dve.memset(carry[:, 1, T - 1:T], -FAR))
                step(dve.tensor_tensor(carry[:, 0, 1:], through[:, 0, 0:T - 1], tile_flags[:, 1, 1:], ALU.add))
                step(dve.tensor_tensor(carry[:, 1, 0:T - 1], through[:, 1, 1:], tile_flags[:, 3, 0:T - 1], ALU.add))
                dve.sem_inc(carry_ready, 1)
                dve.wait_ge(carry_done, 1)
                for k, at in enumerate((0, P - 1)):
                    step(dve.tensor_tensor(turned[:, :, at], ps_carry[:, k * NG:(k + 1) * NG], turned[:, :, at], ALU.max))
                running()
                step(dve.tensor_tensor(left[:], left[:], right[:], ALU.max))
                step(dve.tensor_copy(turned[:, :, 0], kept[:, 0, :]))
                step(dve.tensor_copy(turned[:, :, P - 1], kept[:, 1, :]))
                step(dve.tensor_tensor(turned[:], turned[:], left[:], ALU.subtract))
                dve.sem_inc(shifted, 1)
                dve.wait_ge(written, QUADS)


def sum_messages(layer, weights, sums, table, src_index, dst_local, block_of, iota_row, sems, nc, **_):
    with ExitStack() as ctx:
        sb = allocator(nc, ctx)
        rows = [sb(f"ms_rows{b}", [P, G, DX]) for b in range(UNROLL)]
        index = [sb(f"ms_index{b}", [P, G], I32) for b in range(UNROLL)]
        place = [sb(f"ms_place{b}", [P, G, P]) for b in range(UNROLL)]
        total = [ctx.enter_context(nc.psum_tensor(f"ms_total{b}", [P, 2, BANK], F32)) for b in range(2)]
        (index_ready, index_seen, rows_free, place_ready, weighted, behind, totalled, cleared, added) = names = [nc.alloc_semaphore("ms_" + s) for s in (
            "index_ready", "index_seen", "rows_free", "place_ready", "weighted", "behind", "totalled", "cleared", "added")]
        gathered = [nc.alloc_semaphore(f"ms_gathered{b}") for b in range(UNROLL)]
        sems += names
        with nc.Block() as block:
            @block.gpsimd
            def _(pool):
                pool.memset(sums[:], 0.0).then_inc(cleared, 1)

                def gather(m, b):
                    pool.wait_ge(rows_free, m + 1)
                    pool.tensor_copy(index[b][:], rows_of(src_index, m)).then_inc(index_ready, 1)
                    pool.wait_ge(index_ready, m + 1)
                    pool.sem_inc(index_seen, 1)
                    for j in range(G):
                        pool.indirect_dma_start(rows[b][:, j, :], None, table,
                                                bass.IndirectOffsetOnAxis(index[b][:, j:j + 1], 0)).then_inc(gathered[b], 16)

                for m in range(AHEAD):
                    gather(m, m)
                with pool.Fori(0, NG) as i:
                    for b in range(UNROLL):
                        gather(i * UNROLL + b + AHEAD, (b + AHEAD) % UNROLL)
                for b in range(UNROLL):
                    pool.wait_ge(gathered[b], landed(layer, b, NG + (b < AHEAD)))

            def weights_of(i, b):
                return weights[:, bass.ds(i, 1), :, b * G:(b + 1) * G].rearrange("p o h j -> p j (o h)")

            @block.scalar
            def _(act):
                with act.Fori(0, NG) as i:
                    for b in range(UNROLL):
                        act.wait_ge(gathered[b], landed(layer, b, i + 1))
                        act.activation(rows[b][:, :, D:DX], weights_of(i, b), ACT.Copy).then_inc(behind, 1)

            @block.tensor
            def _(pe):
                pe.sem_inc(rows_free, UNROLL)
                with pe.Fori(0, NG) as i:
                    for b in range(UNROLL):
                        m = i * UNROLL + b
                        pe.wait_ge(place_ready, m + 1)
                        pe.wait_ge(weighted, m + 1)
                        pe.wait_ge(behind, m + 1)
                        pe.wait_ge(added, m + 1)
                        for j in range(G):
                            for half in range(2):
                                last = pe.matmul(total[b % 2][:, half, 0:HALFX], place[b][:, j, :],
                                                 rows[b][:, j, half * HALFX:(half + 1) * HALFX], start=j == 0, stop=j == G - 1)
                        last.then_inc(totalled, 1)
                        pe.wait_ge(totalled, m + 1)
                        pe.sem_inc(rows_free, 1)

            @block.vector
            def _(dve):
                def prepare(m, i, b, round):
                    dve.tensor_tensor(place[b][:], over(iota_row[:, 0:P], G),
                                      rows_of(dst_local, m).unsqueeze(2).broadcast_to([P, G, P]), ALU.is_equal).then_inc(place_ready, 1)
                    dve.wait_ge(gathered[b], landed(layer, b, round + 1))
                    features = rows[b][:, :, 0:D].rearrange("p j (h d) -> p j h d", h=H)
                    dve.tensor_tensor(features, features, weights_of(i, b).unsqueeze(3).broadcast_to([P, G, H, HD]), ALU.mult).then_inc(weighted, 1)

                def add_total(m, b):
                    block_at = dve.value_load(block_of[0:1, bass.ds(m, 1)], min_val=0, max_val=NT - 1)
                    into = sums[:, bass.ds(block_at, 1), :].rearrange("p o (s d) -> p (o s) d", s=2)
                    dve.wait_ge(totalled, m + 1)
                    dve.wait_ge(added, m + 2)
                    dve.tensor_tensor(into, total[b % 2][:, :, 0:HALFX], into, ALU.add).then_inc(added, 1)

                dve.wait_ge(cleared, 1)
                dve.sem_inc(added, 2)
                prepare(0, 0, 0, 0)
                with dve.Fori(0, NG) as i:
                    for b in range(UNROLL):
                        m = i * UNROLL + b
                        n = (b + 1) // UNROLL
                        prepare(m + 1, i + n, (b + 1) % UNROLL, i + n)
                        add_total(m, b)
                dve.wait_ge(added, NM + 2)
                dve.wait_ge(weighted, NM + 1)
                dve.wait_ge(place_ready, NM + 1)


def end_layer(layer, sums, ln_w, ln_b, sems, nc, nodes, **_):
    with ExitStack() as ctx:
        sb = allocator(nc, ctx)
        norm = Norm(sb, "norm1", [nc.alloc_semaphore(s) for s in Norm.names("norm1")])
        gain, offset = sb("el_gain", [P, D]), sb("el_offset", [P, D])
        mean, bend = sb("el_mean", [P, NT, D]), sb("el_bend", [P, NT, D])
        inverse = sb("el_inverse", [P, NT, H])
        loaded, order, mean_ready, below, exp_done, seen = names = [nc.alloc_semaphore("el_" + s) for s in ("loaded", "order", "mean_ready", "below", "exp_done", "seen")]
        sems += [*names, norm.stats_done, norm.var_ready, norm.root_ready, norm.order, norm.applied]
        with nc.Block() as block:
            @block.sync
            def _(sp):
                sp.dma_start(gain[:], ln_w[bass.ds(layer, 1), :].broadcast_to([P, D])).then_inc(loaded, 16)
                sp.dma_start(offset[:], ln_b[bass.ds(layer, 1), :].broadcast_to([P, D])).then_inc(loaded, 16)

            @block.scalar
            def _(act):
                with act.Fori(0, NT) as t:
                    act.wait_ge(mean_ready, t + 1)
                    act.sem_inc(seen, 1)
                    act.activation(rows_of(bend, t), rows_of(mean, t), ACT.Relu, scale=-1.0).then_inc(below, 1)
                    act.wait_ge(below, t + 1)
                    act.sem_inc(seen, 1)
                    act.activation(rows_of(bend, t), rows_of(bend, t), ACT.Exp, scale=-1.0).then_inc(exp_done, 1)
                norm.scalar(act)

            @block.vector
            def _(dve):
                step = Link(dve, order)
                step(dve.tensor_scalar(inverse[:], sums[:, :, D:DX], TINY, None, ALU.max))
                step(dve.reciprocal(inverse[:], inverse[:]))
                with dve.Fori(0, NT) as t:
                    dve.tensor_tensor(rows_of(mean, t).rearrange("p (h d) -> p h d", h=H),
                                      sums[:, bass.ds(t, 1), 0:D].rearrange("p o (h d) -> p (o h) d", h=H),
                                      rows_of(inverse, t).unsqueeze(2).broadcast_to([P, H, HD]), ALU.mult).then_inc(mean_ready, 1)
                with dve.Fori(0, NT) as t:
                    tile_step = Link(dve, order, t * 2 + step.at)
                    dve.wait_ge(exp_done, t + 1)
                    tile_step(dve.scalar_tensor_tensor(rows_of(mean, t), rows_of(mean, t), 0.0, rows_of(bend, t), ALU.max, ALU.add))
                    tile_step(dve.scalar_tensor_tensor(rows_of(nodes, t), rows_of(mean, t), -1.0, rows_of(nodes, t), ALU.add, ALU.add))
                step.at = step.at + 2 * NT
                norm.vector(dve, nodes)
                dve.wait_ge(loaded, 32)
                step(dve.tensor_tensor(nodes[:], nodes[:], over(gain[:], NT), ALU.mult))
                step(dve.tensor_tensor(nodes[:], nodes[:], over(offset[:], NT), ALU.add))


def attention_layers(Wsrc, bsrc, Wdst, bdst, attn, ln_w, ln_b, k):
    nc, sems = k["nc"], []
    with nc.Fori(0, LAYERS) as layer:
        with ExitStack() as ctx:
            sb = allocator(nc, ctx)
            logits = sb("logits", [P, NG + 1, H, TG])
            spare = nc.alloc_semaphore("spare_cleared")
            sems.append(spare)
            with nc.Block() as block:
                @block.vector
                def _(dve):
                    dve.memset(logits[:, NG], 0.0).then_inc(spare, 1)
                    dve.wait_ge(spare, 1)
            with ExitStack() as inner:
                sb = allocator(nc, inner)
                attn_relu = sb("attn_relu", [P, D])
                dst_rows = sb("dst_rows", [P, NT, SPLIT, DX], BF16)
                project(layer, Wsrc, bsrc, Wdst, bdst, attn, attn_relu, dst_rows, sems, **k)
                logits_of_edges(layer, attn=attn, attn_relu=attn_relu, dst_rows=dst_rows, logits=logits, sems=sems, **k)
            softmax_weights(logits=logits, sems=sems, **k)
            sums = allocator(nc, ctx)("sums", [P, NT, DX])
            sum_messages(layer, weights=logits, sums=sums, sems=sems, **k)
            end_layer(layer, sums, ln_w, ln_b, sems, **k)
        with nc.Block() as block:
            @block.sync
            def _(sp):
                for s in sems:
                    sp.sem_clear(s)


def mix(x, W_qkv, b_qkv, W_out, b_out, nc, ident, nodes, row_valid, x_mix, **_):
    W_KV = 2 * D
    with ExitStack() as ctx:
        sb = allocator(nc, ctx)
        nodes_t = sb("mx_nodes_t", [P, KC, NT * P])
        kv_bias = sb("mx_kv_bias", [P, W_KV])
        kv = sb("mx_kv", [P, PAIRS, P + 1])
        with ExitStack() as inner:
            sb = allocator(nc, inner)
            w = sb("mx_w", [P, KC, W_KV])
            node = [sb(f"mx_node{b}", [P, D]) for b in range(2)]
            node_t = [sb(f"mx_node_t{b}", [P, KC, P]) for b in range(2)]
            key, key_low, key_phi = sb("mx_key", [P, D]), sb("mx_key_low", [P, D]), [sb(f"mx_key_phi{b}", [P, D]) for b in range(2)]
            value = [sb(f"mx_value{b}", [P, PAIRS, P + 1]) for b in range(2)]
            turned = inner.enter_context(nc.psum_tensor("mx_turned", [P, 2 * BANK], F32))
            key_ps = inner.enter_context(nc.psum_tensor("mx_key_ps", [P, 2, BANK], F32))
            value_ps = inner.enter_context(nc.psum_tensor("mx_value_ps", [P, 2, BANK], F32))
            kv_ps = inner.enter_context(nc.psum_tensor("mx_kv_ps", [P, 2, BANK], F32))
            (w_loaded, node_ready, turned_done, turned_free, node_t_ready, key_done, key_taken, low_ready, exp_done, value_done,
             value_taken, kv_in, kv_done, kv_taken, order, cleared, node_t_free) = inner.enter_context(signals(nc, ["mx_" + s for s in (
                 "w_loaded", "node_ready", "turned_done", "turned_free", "node_t_ready", "key_done", "key_taken", "low_ready",
                 "exp_done", "value_done", "value_taken", "kv_in", "kv_done", "kv_taken", "order", "cleared", "node_t_free")]))
            STEPS = 7
            with nc.Block() as block:
                @block.sync
                def _(sp):
                    sp.dma_start(w[:], W_qkv[:, D:].rearrange("(c p) n -> p c n", p=P)).then_inc(w_loaded, 16)
                    sp.dma_start(kv_bias[:], b_qkv[D:].rearrange("(o n) -> o n", o=1).broadcast_to([P, W_KV])).then_inc(w_loaded, 16)
                    sp.wait_ge(w_loaded, 32)

                @block.scalar
                def _(act):
                    def copy_node(t, b):
                        act.activation(node[b][:], rows_of(nodes, t), ACT.Copy).then_inc(node_ready, 1)

                    def copy_turned(t, b):
                        act.wait_ge(turned_done, t + 1)
                        act.wait_ge(node_t_free, t + 1)
                        from_ps = turned[:, 0:D].rearrange("p (c n) -> p c n", c=KC)
                        act.activation(node_t[b][:], from_ps, ACT.Copy).then_inc(node_t_ready, 1)
                        act.activation(nodes_t[:, :, bass.ds(t * P, P)], from_ps, ACT.Copy).then_inc(turned_free, 1)

                    def key_exp(t):
                        act.wait_ge(low_ready, t + 1)
                        act.activation(key_low[:], key_low[:], ACT.Exp).then_inc(exp_done, 1)

                    act.sem_inc(turned_free, 1)
                    copy_node(0, 0)
                    copy_turned(0, 0)
                    copy_node(1, 1)
                    with act.Fori(0, NT // 2 - 1) as i:
                        for b in range(2):
                            t = i * 2 + b
                            copy_turned(t + 1, 1 - b)
                            copy_node(t + 2, b)
                            key_exp(t)
                    copy_turned(NT - 1, 1)
                    key_exp(NT - 2)
                    key_exp(NT - 1)

                @block.tensor
                def _(pe):
                    def turn(t, b):
                        pe.wait_ge(node_ready, t + 1)
                        pe.wait_ge(turned_free, t + 1)
                        for c in range(KC):
                            last = pe.transpose(turned[:, c * P:(c + 1) * P], node[b][:, c * P:(c + 1) * P], ident[:])
                        last.then_inc(turned_done, 1)

                    def product(t, b, s, ps, taken, done):
                        pe.wait_ge(taken, t + 1)
                        for half in range(2):
                            at = s * D + half * HALF
                            for c in range(KC):
                                last = pe.matmul(ps[:, half, 0:HALF], node_t[b][:, c, :], w[:, c, at:at + HALF],
                                                 start=c == 0, stop=c == KC - 1)
                        last.then_inc(done, 1)

                    def keys_by_values(t, b):
                        pe.wait_ge(kv_in, t + 1)
                        pe.wait_ge(kv_taken, t + 1)
                        for pair in range(PAIRS):
                            at = pair % 3 * (P + 1)
                            last = pe.matmul(kv_ps[:, pair // 3, at:at + P + 1], key_phi[b][:, pair * P:(pair + 1) * P],
                                             value[b][:, pair, :], start=True, stop=True)
                        last.then_inc(kv_done, 1)

                    def tile(t, b, first=False, final=False):
                        pe.wait_ge(node_t_ready, t + 1)
                        product(t, b, 0, key_ps, key_taken, key_done)
                        if not final:
                            turn(t + 1, 1 - b)
                        product(t, b, 1, value_ps, value_taken, value_done)
                        pe.wait_ge(value_done, t + 1)
                        pe.sem_inc(node_t_free, 1)
                        if not first:
                            keys_by_values(t - 1, 1 - b)

                    pe.sem_inc(node_t_free, 2)
                    turn(0, 0)
                    pe.wait_ge(w_loaded, 32)
                    tile(0, 0, first=True)
                    with pe.Fori(0, NT // 2 - 1) as i:
                        tile(i * 2 + 1, 1)
                        tile(i * 2 + 2, 0)
                    tile(NT - 1, 1, final=True)
                    keys_by_values(NT - 1, 1)

                @block.vector
                def _(dve):
                    for b in range(2):
                        dve.memset(value[b][:, :, P:], 1.0).then_inc(cleared, 1)
                    dve.memset(kv[:], 0.0).then_inc(cleared, 1)
                    for free in (key_taken, value_taken, kv_taken):
                        dve.sem_inc(free, 1)
                    dve.wait_ge(cleared, 3)
                    dve.wait_ge(w_loaded, 32)
                    def add_kv(t, step):
                        dve.wait_ge(kv_done, t + 1)
                        into = kv[:].rearrange("p (s a) d -> p s (a d)", s=2)
                        step(dve.tensor_tensor(into, kv_ps[:, :, 0:3 * (P + 1)], into, ALU.add))
                        dve.sem_inc(kv_taken, 1)

                    def tile(t, b, first=False):
                        step = Link(dve, order, 0) if first else Link(dve, order, t * STEPS - 1)
                        dve.wait_ge(key_done, t + 1)
                        step(dve.tensor_tensor(key[:].rearrange("p (s d) -> p s d", s=2), key_ps[:, :, 0:HALF],
                                               kv_bias[:, 0:D].rearrange("p (s d) -> p s d", s=2), ALU.add))
                        dve.sem_inc(key_taken, 1)
                        step(dve.tensor_scalar(key_low[:], key[:], 0.0, None, ALU.min))
                        dve.sem_inc(low_ready, 1)
                        dve.wait_ge(value_done, t + 1)
                        for half in range(2):
                            at = D + half * HALF
                            step(dve.tensor_tensor(value[b][:, half * 3:half * 3 + 3, 0:P],
                                                   value_ps[:, half, 0:HALF].rearrange("p (a d) -> p a d", a=3),
                                                   kv_bias[:, at:at + HALF].rearrange("p (a d) -> p a d", a=3), ALU.add))
                        dve.sem_inc(value_taken, 1)
                        dve.wait_ge(exp_done, t + 1)
                        step(dve.scalar_tensor_tensor(key_phi[b][:], key[:], 0.0, key_low[:], ALU.max, ALU.add))
                        step(dve.tensor_scalar(key_phi[b][:], key_phi[b][:], row_valid[:, bass.ds(t, 1)], None, ALU.mult))
                        dve.sem_inc(kv_in, 1)
                        if not first:
                            add_kv(t - 1, step)

                    tile(0, 0, first=True)
                    with dve.Fori(0, NT // 2 - 1) as i:
                        tile(i * 2 + 1, 1)
                        tile(i * 2 + 2, 0)
                    tile(NT - 1, 1)
                    add_kv(NT - 1, Link(dve, order, NT * STEPS - 1))
        mixed_t = allocator(nc, ctx)("mx_mixed_t", [P, PAIRS, NT * P])
        with ExitStack() as inner:
            sb = allocator(nc, inner)
            bias = sb("mx_q_bias", [P, PAIRS])
            wq = [sb(f"mx_wq{b}", [P, KC, P]) for b in range(2)]
            pair_kv = [sb(f"mx_pair_kv{b}", [P, P]) for b in range(2)]
            pair_sum = [sb(f"mx_pair_sum{b}", [P, P]) for b in range(2)]
            low, high, query = ([sb(f"mx_{s}{b}", [P, BANK]) for b in range(2)] for s in ("low", "high", "query"))
            den = [sb(f"mx_den{b}", [P, BANK]) for b in range(2)]
            q_ps, num_ps, den_ps = ([inner.enter_context(nc.psum_tensor(f"mx_{s}_ps{b}", [P, BANK], F32)) for b in range(2)]
                                    for s in ("q", "num", "den"))
            (bias_loaded, q_done, q_low, q_exp, q_ready, weighed, out_ready, pair_ready, q_taken, out_taken, order2, wq_free, zeroed) = inner.enter_context(signals(nc, ["mx2_" + s for s in (
                    "bias_loaded", "q_done", "q_low", "q_exp", "q_ready", "weighed", "out_ready", "pair_ready", "q_taken", "out_taken",
                    "order", "wq_free", "zeroed")]))
            wq_loaded = inner.enter_context(signals(nc, [f"mx2_wq_loaded{b}" for b in range(2)]))
            CUTS = [(at, min(BANK, NT * P - at)) for at in range(0, NT * P, BANK)]
            CH = len(CUTS)
            STEPS = 4 + 6 * CH
            with nc.Block() as block:
                @block.sync
                def _(sp):
                    sp.dma_start(bias[:], b_qkv[0:D].rearrange("(f p) -> p f", p=P), allow_slow_non_contiguous=True).then_inc(bias_loaded, 16)
                    with sp.Fori(0, PAIRS // 2) as i:
                        for b in range(2):
                            f = i * 2 + b
                            sp.wait_ge(wq_free, f + 1)
                            sp.dma_start(wq[b][:], W_qkv[:, bass.ds(f * P, P)].rearrange("(c p) n -> p c n", p=P)).then_inc(wq_loaded[b], 16)
                    for b in range(2):
                        sp.wait_ge(wq_loaded[b], 16 * (PAIRS // 2))

                @block.tensor
                def _(pe):
                    def query_products(f, b, i, n):
                        at, size = CUTS[n]
                        r = (b * CH + n) % 2
                        if n == 0:
                            pe.wait_ge(wq_loaded[b], 16 * (i + 1))
                        pe.wait_ge(q_taken, f * CH + n + 1)
                        for c in range(KC):
                            last = pe.matmul(q_ps[r][:, 0:size], wq[b][:, c, :], nodes_t[:, c, at:at + size], start=c == 0, stop=c == KC - 1)
                        last.then_inc(q_done, 1)

                    def pairs(i, final=False):
                        for b in range(2):
                            f = i * 2 + b
                            for n, (at, size) in enumerate(CUTS):
                                r = (b * CH + n) % 2
                                if n + 1 < CH:
                                    query_products(f, b, i, n + 1)
                                elif not (final and b == 1):
                                    query_products(f + 1, 1 - b, i + b, 0)
                                if n == 0:
                                    pe.wait_ge(pair_ready, f + 1)
                                pe.wait_ge(q_ready, f * CH + n + 1)
                                pe.wait_ge(out_taken, f * CH + n + 1)
                                pe.matmul(num_ps[r][:, 0:size], pair_kv[b][:], query[r][:, 0:size], start=True, stop=True)
                                pe.matmul(den_ps[r][:, 0:size], pair_sum[b][:], query[r][:, 0:size], start=True, stop=True).then_inc(weighed, 1)
                            pe.wait_ge(weighed, f * CH + CH)
                            pe.sem_inc(wq_free, 1)

                    pe.sem_inc(wq_free, 2)
                    query_products(0, 0, 0, 0)
                    with pe.Fori(0, PAIRS // 2 - 1) as i:
                        pairs(i)
                    pairs(PAIRS // 2 - 1, final=True)

                @block.scalar
                def _(act):
                    with act.Fori(0, PAIRS // 2) as i:
                        for b in range(2):
                            f = i * 2 + b
                            for n, (at, size) in enumerate(CUTS):
                                r = (b * CH + n) % 2
                                act.wait_ge(q_low, f * CH + n + 1)
                                act.activation(low[r][:, 0:size], low[r][:, 0:size], ACT.Exp).then_inc(q_exp, 1)

                @block.vector
                def _(dve):
                    dve.sem_inc(q_taken, 2)
                    dve.sem_inc(out_taken, 2)
                    for b in range(2):
                        dve.memset(pair_kv[b][:], 0.0).then_inc(zeroed, 1)
                        dve.memset(pair_sum[b][:], 0.0).then_inc(zeroed, 1)
                    dve.wait_ge(zeroed, 4)
                    dve.wait_ge(bias_loaded, 16)
                    def clip(f, b, n, step):
                        size = CUTS[n][1]
                        r = (b * CH + n) % 2
                        dve.wait_ge(q_done, f * CH + n + 1)
                        step(dve.tensor_scalar(low[r][:, 0:size], q_ps[r][:, 0:size], bias[:, bass.ds(f, 1)], 0.0, ALU.add, ALU.min))
                        dve.sem_inc(q_low, 1)
                        step(dve.tensor_scalar(high[r][:, 0:size], q_ps[r][:, 0:size], bias[:, bass.ds(f, 1)], 0.0, ALU.add, ALU.max))
                        dve.sem_inc(q_taken, 1)

                    def pairs(i, final=False):
                        for b in range(2):
                            f = i * 2 + b
                            step = Link(dve, order2, f * STEPS + 2)
                            for a in range(0, P, MIX_D):
                                head = kv[a:a + MIX_D, bass.ds(f, 1), :].rearrange("p o d -> p (o d)")
                                step(dve.tensor_copy(pair_kv[b][a:a + MIX_D, a:a + MIX_D], head[:, a:a + MIX_D]))
                                step(dve.tensor_copy(pair_sum[b][a:a + MIX_D, a:a + MIX_D], head[:, P:P + 1].broadcast_to([MIX_D, MIX_D])))
                            dve.sem_inc(pair_ready, 1)
                            for n, (at, size) in enumerate(CUTS):
                                r = (b * CH + n) % 2
                                dve.wait_ge(q_exp, f * CH + n + 1)
                                step(dve.tensor_tensor(query[r][:, 0:size], high[r][:, 0:size], low[r][:, 0:size], ALU.add))
                                dve.sem_inc(q_ready, 1)
                                if n + 1 < CH:
                                    clip(f, b, n + 1, step)
                                elif not (final and b == 1):
                                    clip(f + 1, 1 - b, 0, step)
                                dve.wait_ge(weighed, f * CH + n + 1)
                                step(dve.tensor_scalar(den[r][:, 0:size], den_ps[r][:, 0:size], MIX_EPS, None, ALU.max))
                                step(dve.reciprocal(den[r][:, 0:size], den[r][:, 0:size]))
                                step(dve.tensor_tensor(mixed_t[:, bass.ds(f, 1), at:at + size].rearrange("p o n -> p (o n)"),
                                                       num_ps[r][:, 0:size], den[r][:, 0:size], ALU.mult))
                                dve.sem_inc(out_taken, 1)

                    clip(0, 0, 0, Link(dve, order2))
                    with dve.Fori(0, PAIRS // 2 - 1) as i:
                        pairs(i)
                    pairs(PAIRS // 2 - 1, final=True)
        total = nodes_t[:].rearrange("p c n -> p (c n)").rearrange("p (t d) -> p t d", t=NT)
        with ExitStack() as inner:
            sb = allocator(nc, inner)
            w = sb("mx_wo", [P, KC, D])
            bias = sb("mx_bo", [P, D])
            part = [sb(f"mx_part{b}", [P, KC, P]) for b in range(2)]
            ps = [inner.enter_context(nc.psum_tensor(f"mx_out_ps{b}", [P, 2, BANK], F32)) for b in range(2)]
            w_loaded, x_loaded, part_ready, done, taken, order3, zeroed3, stored = inner.enter_context(signals(nc, ["mx3_" + s for s in (
                "w_loaded", "x_loaded", "part_ready", "done", "taken", "order", "zeroed", "stored")]))
            with nc.Block() as block:
                @block.sync
                def _(sp):
                    sp.dma_start(w[:], W_out.rearrange("(c p) n -> p c n", p=P)).then_inc(w_loaded, 16)
                    sp.dma_start(bias[:], b_out.rearrange("(o n) -> o n", o=1).broadcast_to([P, D])).then_inc(w_loaded, 16)
                    sp.dma_start(total[:, 0:FULL, :], x[0:FULL * P, :].rearrange("(t p) d -> p t d", p=P)).then_inc(x_loaded, 16)
                    sp.wait_ge(zeroed3, 1)
                    sp.dma_start(total[0:LAST, FULL, :], x[FULL * P:N, :]).then_inc(x_loaded, 16)
                    sp.wait_ge(order3, 2 * NT)
                    sp.dma_start(x_mix, total.rearrange("p t d -> p (t d)")).then_inc(stored, 16)
                    sp.wait_ge(stored, 16)

                @block.scalar
                def _(act):
                    with act.Fori(0, NT // 2) as i:
                        for b in range(2):
                            t = i * 2 + b
                            act.wait_ge(taken, t + 1)
                            act.activation(part[b][:], mixed_t[:, :, bass.ds(t * P, P)], ACT.Copy).then_inc(part_ready, 1)

                @block.tensor
                def _(pe):
                    pe.wait_ge(w_loaded, 32)
                    with pe.Fori(0, NT // 2) as i:
                        for b in range(2):
                            t = i * 2 + b
                            pe.wait_ge(part_ready, t + 1)
                            for half in range(2):
                                for c in range(KC):
                                    last = pe.matmul(ps[b][:, half, 0:HALF], part[b][:, c, :], w[:, c, half * HALF:(half + 1) * HALF],
                                                     start=c == 0, stop=c == KC - 1)
                            last.then_inc(done, 1)

                @block.vector
                def _(dve):
                    dve.memset(total[:, FULL, :], 0.0).then_inc(zeroed3, 1)
                    dve.sem_inc(taken, 2)
                    dve.wait_ge(x_loaded, 32)
                    dve.wait_ge(w_loaded, 32)
                    with dve.Fori(0, NT // 2) as i:
                        for b in range(2):
                            t = i * 2 + b
                            step = Link(dve, order3, t * 2)
                            row = rows_of(total, t)
                            step(dve.tensor_tensor(row, row, bias[:], ALU.add))
                            dve.wait_ge(done, t + 1)
                            halves = row.rearrange("p (s d) -> p s d", s=2)
                            step(dve.tensor_tensor(halves, ps[b][:, :, 0:HALF], halves, ALU.add))
                            dve.sem_inc(taken, 1)


def finish(on_w, on_b, in_weight, in_bias, out_weight, out, nc, ident, nodes, x_mix, **_):
    with ExitStack() as ctx:
        sb = allocator(nc, ctx)
        norm_h, norm_y = (Norm(sb, name, ctx.enter_context(signals(nc, Norm.names(name)))) for name in ("norm2", "norm3"))
        gain, offset = sb("fi_gain", [P, D]), sb("fi_offset", [P, D])
        y = sb("fi_y", [P, NT, D])
        w_in_rows = sb("fi_w_in_rows", [P, HC, D])
        w_in = sb("fi_w_in", [P, KC, HID])
        w_out = sb("fi_w_out", [P, HC, D])
        bias = sb("fi_bias", [P, HC])
        node = [sb(f"fi_node{b}", [P, D]) for b in range(2)]
        node_t = [sb(f"fi_node_t{b}", [P, KC, P]) for b in range(2)]
        hidden = [sb(f"fi_hidden{b}", [P, HC, P]) for b in range(2)]
        turned = ctx.enter_context(nc.psum_tensor("fi_turned", [P, 2 * BANK], F32))
        hidden_ps = [ctx.enter_context(nc.psum_tensor(f"fi_hidden_ps{b}", [P, BANK], F32)) for b in range(2)]
        out_ps = [ctx.enter_context(nc.psum_tensor(f"fi_out_ps{b}", [P, 2, BANK], F32)) for b in range(2)]
        (affine_loaded, y_loaded, w_loaded, w_turned, w_ready, normed, order, node_ready, turned_done, node_t_ready, hidden_done,
         hidden_ready, out_done, out_taken, stored) = ctx.enter_context(signals(nc, ["fi_" + s for s in (
             "affine_loaded", "y_loaded", "w_loaded", "w_turned", "w_ready", "normed", "order", "node_ready", "turned_done",
             "node_t_ready", "hidden_done", "hidden_ready", "out_done", "out_taken", "stored")]))
        with nc.Block() as block:
            @block.sync
            def _(sp):
                for to, what in ((gain, on_w), (offset, on_b)):
                    sp.dma_start(to[:], what.rearrange("(o n) -> o n", o=1).broadcast_to([P, D])).then_inc(affine_loaded, 16)
                sp.dma_start(y[:].rearrange("p t d -> p (t d)"), x_mix).then_inc(y_loaded, 16)
                sp.dma_start(w_in_rows[:], in_weight.rearrange("(c p) n -> p c n", p=P)).then_inc(w_loaded, 16)
                sp.dma_start(w_out[:], out_weight.rearrange("(c p) n -> p c n", p=P)).then_inc(w_loaded, 16)
                sp.dma_start(bias[:], in_bias.rearrange("(c p) -> p c", p=P), allow_slow_non_contiguous=True).then_inc(w_loaded, 16)
                sp.wait_ge(out_taken, NT + 2)
                sp.dma_start(out[0:FULL * P, :].rearrange("(t p) d -> p t d", p=P), y[:, 0:FULL, :]).then_inc(stored, 16)
                sp.dma_start(out[FULL * P:N, :], y[0:LAST, FULL, :]).then_inc(stored, 16)
                sp.wait_ge(stored, 32)

            @block.scalar
            def _(act):
                for c in range(HC):
                    act.wait_ge(w_turned, c + 1)
                    act.activation(w_in[:, :, c * P:(c + 1) * P], turned[:, 0:D].rearrange("p (c n) -> p c n", c=KC), ACT.Copy).then_inc(w_ready, 1)
                norm_h.scalar(act)
                norm_y.scalar(act)
                act.wait_ge(normed, 1)
                with act.Fori(0, NT // 2) as i:
                    for b in range(2):
                        t = i * 2 + b
                        act.activation(node[b][:], rows_of(nodes, t), ACT.Copy).then_inc(node_ready, 1)
                        act.wait_ge(turned_done, t + 1)
                        act.activation(node_t[b][:], turned[:, 0:D].rearrange("p (c n) -> p c n", c=KC), ACT.Copy).then_inc(node_t_ready, 1)
                        act.wait_ge(hidden_done, t + 1)
                        for c in range(HC):
                            act.activation(hidden[b][:, c, :], hidden_ps[b][:, c * P:(c + 1) * P], ACT.Gelu, bias=bias[:, c:c + 1]).then_inc(hidden_ready, 1)

            @block.tensor
            def _(pe):
                pe.wait_ge(w_loaded, 48)
                for c in range(HC):
                    if c:
                        pe.wait_ge(w_ready, c)
                    for n in range(KC):
                        last = pe.transpose(turned[:, n * P:(n + 1) * P], w_in_rows[:, c, n * P:(n + 1) * P], ident[:])
                    last.then_inc(w_turned, 1)
                pe.wait_ge(w_ready, HC)
                with pe.Fori(0, NT // 2) as i:
                    for b in range(2):
                        t = i * 2 + b
                        pe.wait_ge(node_ready, t + 1)
                        for c in range(KC):
                            last = pe.transpose(turned[:, c * P:(c + 1) * P], node[b][:, c * P:(c + 1) * P], ident[:])
                        last.then_inc(turned_done, 1)
                        pe.wait_ge(node_t_ready, t + 1)
                        for n in range(HC):
                            for c in range(KC):
                                last = pe.matmul(hidden_ps[b][:, n * P:(n + 1) * P], w_in[:, c, n * P:(n + 1) * P], node_t[b][:, c, :],
                                                 start=c == 0, stop=c == KC - 1)
                        last.then_inc(hidden_done, 1)
                        pe.wait_ge(hidden_ready, HC * (t + 1))
                        pe.wait_ge(out_taken, t + 1)
                        for half in range(2):
                            for c in range(HC):
                                last = pe.matmul(out_ps[b][:, half, 0:HALF], hidden[b][:, c, :], w_out[:, c, half * HALF:(half + 1) * HALF],
                                                 start=c == 0, stop=c == HC - 1)
                        last.then_inc(out_done, 1)

            @block.vector
            def _(dve):
                step = Link(dve, order)
                norm_h.vector(dve, nodes)
                dve.wait_ge(affine_loaded, 32)
                step(dve.tensor_tensor(nodes[:], nodes[:], over(gain[:], NT), ALU.mult))
                step(dve.tensor_tensor(nodes[:], nodes[:], over(offset[:], NT), ALU.add))
                dve.wait_ge(y_loaded, 16)
                step(dve.tensor_tensor(y[:], y[:], nodes[:], ALU.add))
                step(dve.tensor_copy(nodes[:], y[:]))
                norm_y.vector(dve, nodes)
                dve.sem_inc(normed, 1)
                dve.sem_inc(out_taken, 2)
                with dve.Fori(0, NT // 2) as i:
                    for b in range(2):
                        t = i * 2 + b
                        dve.wait_ge(out_done, t + 1)
                        row = rows_of(y, t).rearrange("p (s d) -> p s d", s=2)
                        dve.tensor_tensor(row, out_ps[b][:, :, 0:HALF], row, ALU.add).then_inc(out_taken, 1)


def program(nc, x, src, dst, Wsrc, bsrc, Wdst, bdst, attn, ln_w, ln_b, on_w, on_b, W_qkv, b_qkv, W_out, b_out,
            in_weight, in_bias, out_weight, out):
    with ExitStack() as ctx:
        k = persistent(nc, allocator(nc, ctx))
        load_and_norm(x, **k)
        mix(x, W_qkv, b_qkv, W_out, b_out, **k)
        pad_and_check(src, dst, **k)
        sort_edges(src, dst, **k)
        index_edges(dst, **k)
        attention_layers(Wsrc, bsrc, Wdst, bdst, attn, ln_w, ln_b, k)
        finish(on_w, on_b, in_weight, in_bias, out_weight, out, **k)


_INS = (['x', 'src', 'dst']
        + ['L0_gnn_' + n for n in ('Wsrc', 'bsrc', 'Wdst', 'bdst', 'attn', 'ln_w', 'ln_b', 'on_w', 'on_b')]
        + ['L0_mix_' + n for n in ('W_qkv', 'b_qkv', 'W_out', 'b_out')]
        + ['L0_ffn_' + n for n in ('in_weight', 'in_bias', 'out_weight')])


def kernel(**inputs):
    import numpy as _np
    import concourse.bacc as _bacc
    from concourse import mybir as _mybir
    from concourse.bass_utils import run_bass_kernel_spmd as _run

    nc = _bacc.Bacc("TRN2", target_bir_lowering=False, num_devices=1)
    arrays, args = {}, []
    for name in _INS:
        a = _np.ascontiguousarray(inputs[name])
        arrays[f"in_{name}"] = a
        args.append(nc.dram_tensor(f"in_{name}", a.shape, _mybir.dt.from_np(a.dtype), kind="ExternalInput").ap())
    out = nc.dram_tensor("out_0", (N, D), F32, kind="ExternalOutput").ap()
    program(nc, *args, out)
    r = _run(nc, [arrays], core_ids=[0])
    return r.results[0]["out_0"]
```
